# Optimizing a Trainium2 kernel written in Bass

```python
import numpy as np
import jax
import jax.numpy as jnp

def _softmax(x, axis=-1):
    return jax.nn.softmax(x, axis=axis)

def _gelu(x):
    return jax.nn.gelu(x, approximate=True)

def _silu(x):
    return jax.nn.silu(x)

def _sigmoid(x):
    return jax.nn.sigmoid(x)

def _layernorm(x, axis=-1, eps=1e-05):
    m = jnp.mean(x, axis=axis, keepdims=True)
    v = jnp.var(x, axis=axis, keepdims=True)
    return (x - m) / jnp.sqrt(v + eps)

def _scatter_add(tgt, idx, src, axis=0):
    return tgt.at[idx].add(src)

def _segment_sum(src, seg, n):
    return jax.ops.segment_sum(src, seg, n)
kernel_name = 'mk_recurrent_d1_jaxref_r8_dc89c3'

def setup_inputs(seed: int=0):
    np.random.seed(seed)
    _w = jnp.asarray

    def _L0_attn_setup():
        import jax, jax.numpy as jnp
        import numpy as np
        D_MODEL = 128
        D_FF = 512
        FFN_H = int(2 * D_FF / 3)
        B, S = (4, 512)
        LN_EPS = 1e-05
        ATTN_EPS = 1e-06

        def layer_norm(x, g, b):
            mu = jnp.mean(x, axis=-1, keepdims=True)
            var = jnp.mean(jnp.square(x - mu), axis=-1, keepdims=True)
            return (x - mu) * jax.lax.rsqrt(var + LN_EPS) * g + b
        key = jax.random.key(seed)
        ks = jax.random.split(key, 16)
        s = 0.02
        return {'x': jax.random.normal(ks[0], (B, S, D_MODEL), dtype=jnp.float32), 'Wqkv': jax.random.normal(ks[1], (D_MODEL, 3 * D_MODEL), dtype=jnp.float32) * s, 'bqkv': jnp.zeros((3 * D_MODEL,), jnp.float32), 'Wg': jax.random.normal(ks[2], (D_MODEL, FFN_H), dtype=jnp.float32) * s, 'bg': jnp.zeros((FFN_H,), jnp.float32), 'Wu': jax.random.normal(ks[3], (D_MODEL, FFN_H), dtype=jnp.float32) * s, 'bu': jnp.zeros((FFN_H,), jnp.float32), 'Wd': jax.random.normal(ks[4], (FFN_H, D_MODEL), dtype=jnp.float32) * s, 'bd': jnp.zeros((D_MODEL,), jnp.float32), 'g1': jnp.ones((D_MODEL,), jnp.float32), 'b1': jnp.zeros((D_MODEL,), jnp.float32), 'g2': jnp.ones((D_MODEL,), jnp.float32), 'b2': jnp.zeros((D_MODEL,), jnp.float32)}
    _L0_attn_in = _L0_attn_setup()

    def _L0_ffn_setup():
        import jax, jax.numpy as jnp
        import numpy as np
        B, S, DIM = (4, 512, 128)
        BASE_COUPLING = 0.1
        NUM_CYCLES = 3

        def _gelu(x):
            return jax.nn.gelu(x, approximate=False)

        def _coupling_net(h, w1, b1, w2, b2, w3, b3, w4, b4):
            h = _gelu(h @ w1 + b1)
            h = _gelu(h @ w2 + b2)
            h = _gelu(h @ w3 + b3)
            return jax.nn.sigmoid(h @ w4 + b4)

        def _global_net(h, w1, b1, w2, b2, w3, b3):
            h = _gelu(h @ w1 + b1)
            h = _gelu(h @ w2 + b2)
            return jax.nn.sigmoid(h @ w3 + b3)

        def _twist(x):
            o_r, o_i, p_r, p_i = jnp.split(x, 4, axis=-1)
            return jnp.concatenate([p_r, -p_i, -o_r, o_i], axis=-1)
        key = jax.random.key(seed)
        ks = jax.random.split(key, 9)
        d = DIM

        def w(k, fan_in, fan_out):
            return jax.random.normal(k, (fan_in, fan_out), dtype=jnp.float32) / np.sqrt(fan_in).astype(np.float32)
        inp = {'x': jax.random.normal(ks[0], (B, S, d), dtype=jnp.float32)}
        cn_dims = [(d, d), (d, d // 2), (d // 2, d // 4), (d // 4, 1)]
        for i, (a, b) in enumerate(cn_dims):
            inp[f'cn_w{i + 1}'] = w(ks[1 + i], a, b)
            inp[f'cn_b{i + 1}'] = jnp.zeros((b,), dtype=jnp.float32)
        gc_dims = [(d, d // 2), (d // 2, d // 4), (d // 4, 1)]
        for i, (a, b) in enumerate(gc_dims):
            inp[f'gc_w{i + 1}'] = w(ks[5 + i], a, b)
            inp[f'gc_b{i + 1}'] = jnp.zeros((b,), dtype=jnp.float32)
        inp['adaptive_range'] = jnp.full((1,), 0.2, dtype=jnp.float32)
        return inp
    _L0_ffn_in = _L0_ffn_setup()
    _d = {'L0_attn_x': _L0_attn_in['x'], 'L0_attn_Wqkv': _L0_attn_in['Wqkv'], 'L0_attn_bqkv': _L0_attn_in['bqkv'], 'L0_attn_Wg': _L0_attn_in['Wg'], 'L0_attn_bg': _L0_attn_in['bg'], 'L0_attn_Wu': _L0_attn_in['Wu'], 'L0_attn_bu': _L0_attn_in['bu'], 'L0_attn_Wd': _L0_attn_in['Wd'], 'L0_attn_bd': _L0_attn_in['bd'], 'L0_attn_g1': _L0_attn_in['g1'], 'L0_attn_b1': _L0_attn_in['b1'], 'L0_attn_g2': _L0_attn_in['g2'], 'L0_attn_b2': _L0_attn_in['b2'], 'L0_ffn_cn_w1': _L0_ffn_in['cn_w1'], 'L0_ffn_cn_b1': _L0_ffn_in['cn_b1'], 'L0_ffn_cn_w2': _L0_ffn_in['cn_w2'], 'L0_ffn_cn_b2': _L0_ffn_in['cn_b2'], 'L0_ffn_cn_w3': _L0_ffn_in['cn_w3'], 'L0_ffn_cn_b3': _L0_ffn_in['cn_b3'], 'L0_ffn_cn_w4': _L0_ffn_in['cn_w4'], 'L0_ffn_cn_b4': _L0_ffn_in['cn_b4'], 'L0_ffn_gc_w1': _L0_ffn_in['gc_w1'], 'L0_ffn_gc_b1': _L0_ffn_in['gc_b1'], 'L0_ffn_gc_w2': _L0_ffn_in['gc_w2'], 'L0_ffn_gc_b2': _L0_ffn_in['gc_b2'], 'L0_ffn_gc_w3': _L0_ffn_in['gc_w3'], 'L0_ffn_gc_b3': _L0_ffn_in['gc_b3'], 'L0_ffn_adaptive_range': _L0_ffn_in['adaptive_range']}
    _x0 = _d['L0_attn_x']
    _d['L0_attn_x'] = jax.random.normal(jax.random.fold_in(jax.random.key(seed), 1), (8, 512, 128), dtype=_x0.dtype)
    del _x0
    return _d

def reference(L0_attn_x, L0_attn_Wqkv, L0_attn_bqkv, L0_attn_Wg, L0_attn_bg, L0_attn_Wu, L0_attn_bu, L0_attn_Wd, L0_attn_bd, L0_attn_g1, L0_attn_b1, L0_attn_g2, L0_attn_b2, L0_ffn_cn_w1, L0_ffn_cn_b1, L0_ffn_cn_w2, L0_ffn_cn_b2, L0_ffn_cn_w3, L0_ffn_cn_b3, L0_ffn_cn_w4, L0_ffn_cn_b4, L0_ffn_gc_w1, L0_ffn_gc_b1, L0_ffn_gc_w2, L0_ffn_gc_b2, L0_ffn_gc_w3, L0_ffn_gc_b3, L0_ffn_adaptive_range):

    def _L0_attn_ref(x, Wqkv, bqkv, Wg, bg, Wu, bu, Wd, bd, g1, b1, g2, b2):
        import jax, jax.numpy as jnp
        import numpy as np
        D_MODEL = 128
        D_FF = 512
        FFN_H = int(2 * D_FF / 3)
        B, S = (4, 512)
        LN_EPS = 1e-05
        ATTN_EPS = 1e-06

        def layer_norm(x, g, b):
            mu = jnp.mean(x, axis=-1, keepdims=True)
            var = jnp.mean(jnp.square(x - mu), axis=-1, keepdims=True)
            return (x - mu) * jax.lax.rsqrt(var + LN_EPS) * g + b
        qkv = jnp.einsum('bsd,de->bse', x, Wqkv) + bqkv
        q, k, v = jnp.split(qkv, 3, axis=-1)
        qp = jax.nn.elu(q) + 1.0
        kp = jax.nn.elu(k) + 1.0
        kv = jnp.einsum('bsd,bse->bde', kp, v)
        num = jnp.einsum('bsd,bde->bse', qp, kv)
        k_sum = jnp.sum(kp, axis=1)
        den = jnp.einsum('bsd,bd->bs', qp, k_sum)[..., None]
        attn = num / (den + ATTN_EPS)
        x = layer_norm(x + attn, g1, b1)
        gate = jnp.einsum('bsd,dh->bsh', x, Wg) + bg
        up = jnp.einsum('bsd,dh->bsh', x, Wu) + bu
        ffn = jnp.einsum('bsh,hd->bsd', jax.nn.silu(gate) * up, Wd) + bd
        return layer_norm(x + ffn, g2, b2)

    def _L0_ffn_ref(x, cn_w1, cn_b1, cn_w2, cn_b2, cn_w3, cn_b3, cn_w4, cn_b4, gc_w1, gc_b1, gc_w2, gc_b2, gc_w3, gc_b3, adaptive_range):
        import jax, jax.numpy as jnp
        import numpy as np
        B, S, DIM = (4, 512, 128)
        BASE_COUPLING = 0.1
        NUM_CYCLES = 3

        def _gelu(x):
            return jax.nn.gelu(x, approximate=False)

        def _coupling_net(h, w1, b1, w2, b2, w3, b3, w4, b4):
            h = _gelu(h @ w1 + b1)
            h = _gelu(h @ w2 + b2)
            h = _gelu(h @ w3 + b3)
            return jax.nn.sigmoid(h @ w4 + b4)

        def _global_net(h, w1, b1, w2, b2, w3, b3):
            h = _gelu(h @ w1 + b1)
            h = _gelu(h @ w2 + b2)
            return jax.nn.sigmoid(h @ w3 + b3)

        def _twist(x):
            o_r, o_i, p_r, p_i = jnp.split(x, 4, axis=-1)
            return jnp.concatenate([p_r, -p_i, -o_r, o_i], axis=-1)
        global_context = x.mean(axis=1, keepdims=True)
        gf = _global_net(global_context, gc_w1, gc_b1, gc_w2, gc_b2, gc_w3, gc_b3)
        out = x
        for _ in range(NUM_CYCLES):
            tf = _coupling_net(out, cn_w1, cn_b1, cn_w2, cn_b2, cn_w3, cn_b3, cn_w4, cn_b4)
            combined = 0.7 * gf + 0.3 * tf
            coupling = BASE_COUPLING + adaptive_range * (combined - 0.5) * 2.0
            out = out + coupling * _twist(out)
        return out
    x = L0_attn_x
    xn = _layernorm(x, axis=-1)
    s = _L0_attn_ref(xn, L0_attn_Wqkv, L0_attn_bqkv, L0_attn_Wg, L0_attn_bg, L0_attn_Wu, L0_attn_bu, L0_attn_Wd, L0_attn_bd, L0_attn_g1, L0_attn_b1, L0_attn_g2, L0_attn_b2)
    g = _silu(_L0_ffn_ref(xn, L0_ffn_cn_w1, L0_ffn_cn_b1, L0_ffn_cn_w2, L0_ffn_cn_b2, L0_ffn_cn_w3, L0_ffn_cn_b3, L0_ffn_cn_w4, L0_ffn_cn_b4, L0_ffn_gc_w1, L0_ffn_gc_b1, L0_ffn_gc_w2, L0_ffn_gc_b2, L0_ffn_gc_w3, L0_ffn_gc_b3, L0_ffn_adaptive_range))
    x = x + s * g
    return x

_drawn_inputs = setup_inputs


def setup_inputs(seed=0):
    import zlib

    import numpy as np

    out = dict(_drawn_inputs(seed))
    spreads = {'L0_attn_bqkv': (0.0, 0.1),
     'L0_attn_bg': (0.0, 0.8),
     'L0_attn_bu': (0.0, 0.8),
     'L0_attn_bd': (0.0, 1.529),
     'L0_attn_g1': (1.0, 0.2),
     'L0_attn_b1': (0.0, 0.1),
     'L0_attn_g2': (1.0, 0.2),
     'L0_attn_b2': (0.0, 0.1),
     'L0_ffn_cn_b1': (0.0, 0.8),
     'L0_ffn_cn_b2': (0.0, 2.0),
     'L0_ffn_cn_b3': (0.0, 2.0),
     'L0_ffn_gc_b1': (0.0, 0.8),
     'L0_ffn_gc_b2': (0.0, 2.0)}
    factors = {'L0_attn_Wqkv': 8.0,
     'L0_attn_Wg': 8.0,
     'L0_attn_Wu': 8.0,
     'L0_attn_Wd': 8.0,
     'L0_ffn_cn_w1': 8.0,
     'L0_ffn_cn_w2': 8.0,
     'L0_ffn_cn_w3': 8.0,
     'L0_ffn_cn_w4': 5.28,
     'L0_ffn_gc_w1': 64.0,
     'L0_ffn_gc_w2': 64.0,
     'L0_ffn_gc_w3': 8.0}
    for name, (base, spread) in spreads.items():
        noise = np.random.default_rng([zlib.crc32(name.encode()), seed]).standard_normal(out[name].shape)
        drawn = base * np.exp(spread * noise) if base else spread * noise
        out[name] = jnp.asarray(drawn.astype(out[name].dtype))
    for name, factor in factors.items():
        out[name] = (out[name] * factor).astype(out[name].dtype)
    return out
```

```python
from contextlib import ExitStack

import concourse.bass as bass
from concourse import mybir

F32 = mybir.dt.float32
F32R = mybir.dt.float32r
BF16 = mybir.dt.bfloat16
ALU = mybir.AluOpType
ACT = mybir.ActivationFunctionType

P = 128
BATCHES, SEQ, D = 8, 512, 128
TILES = SEQ // P
NTILE = BATCHES * TILES
HID = 2 * 512 // 3
CHUNKS = -(-HID // P)
CHUNK_ROWS = [min(P, HID - c * P) for c in range(CHUNKS)]
PAIRS = BATCHES // 2
CYCLES = 3
SLOTS = CYCLES * PAIRS
LN_EPS, ATTN_EPS = 1e-5, 1e-6
BASE_COUPLING, W_GLOBAL, W_TOKEN = 0.1, 0.7, 0.3
BLK = D // 4

COLS = ["cn_b1", "cn_b2", "cn_b3", "cn_b4", "range", "gc_b1", "gc_b2", "gc_b3", "g1", "b1"] + \
    [f"bg{c}" for c in range(CHUNKS)] + [f"bu{c}" for c in range(CHUNKS)]
COL = {name: i for i, name in enumerate(COLS)}
SMALL = {"cn_w2": 64, "cn_w3": 64, "cn_w4": 4, "gc_w1": 64, "gc_w2": 32, "gc_w3": P, "eye": P}
SMALL_AT = {n: sum(list(SMALL.values())[:i]) for i, n in enumerate(SMALL)}


def gated_block(nc, x, w_first, w_small, w_ffn, w_down, cols, rows, out):
    x_dram = x.rearrange("b (p t) d -> b p (t d)", t=TILES)
    out_dram = out.rearrange("b (p t) d -> b p (t d)", t=TILES)

    with ExitStack() as ctx:
        def sb(name, shape, dt=F32):
            return ctx.enter_context(nc.sbuf_tensor(name, shape, dt))

        def sem(name):
            return ctx.enter_context(nc.semaphore(name))

        first_hi, first_lo = sb("first_hi", [P, 640], F32R), sb("first_lo", [P, 640], F32R)
        small = sb("small", [P, sum(SMALL.values())])
        ffn_hi, ffn_lo = sb("ffn_hi", [P, 2 * HID], F32R), sb("ffn_lo", [P, 2 * HID], F32R)
        wd = sb("wd", [P, CHUNKS, D])
        col = sb("col", [P, len(COLS)])
        row = sb("row", [P, 384 + 5 * D])
        bias3 = sb("bias3", [P, 384 + D], BF16)
        ones_bf = sb("ones_bf", [P, SEQ], BF16)
        sign = sb("sign", [P, 1])
        minus_one = sb("minus_one", [P, 1])
        minus_half = sb("minus_half", [P, TILES])
        half_b4 = sb("half_b4", [P, 1])
        half_gb3 = sb("half_gb3", [P, 1])
        gain = sb("gain", [P, 2])
        bffn = sb("bffn", [P, 2 * CHUNKS])

        eye = small[:, SMALL_AT["eye"]:SMALL_AT["eye"] + P]

        def sm(name, rows_=P):
            return small[0:rows_, SMALL_AT[name]:SMALL_AT[name] + SMALL[name]]

        row_bqkv, row_bd, row_b1 = row[:, 0:384], row[:, 384:512], row[:, 512:640]
        row_g1, row_g2, row_b2 = row[:, 640:768], row[:, 768:896], row[:, 896:1024]

        x_tok = sb("x_tok", [P, BATCHES, TILES, D])
        xn_tok = sb("xn_tok", [P, BATCHES, TILES, D])
        tx_tok = sb("tx_tok", [P, BATCHES, TILES, D])
        pq = sb("pq", [P, NTILE, 2, D])
        r_tok = sb("r_tok", [P, NTILE, D])
        r_flat = r_tok[:, :, :].rearrange("p n d -> p (n d)")
        first_raw = r_flat[:, 0:640]
        ffn_raw = r_flat[:, 640:640 + 2 * HID]
        ffn_scaled = r_flat[:, 1344:1344 + 2 * HID]
        bias_rest = r_flat[:, 2048:2560]
        bias_b = r_flat[:, 2560:2816].bitcast(BF16)
        x1g = sb("x1g", [P, BATCHES, TILES, D])
        x1_hi, x1_lo = sb("x1_hi", [P, BATCHES, SEQ], F32R), sb("x1_lo", [P, BATCHES, SEQ], F32R)

        xT_hi, xT_lo = sb("xT_hi", [P, 2, SEQ], F32R), sb("xT_lo", [P, 2, SEQ], F32R)
        q_stage = sb("q_stage", [P, 2, 2, SEQ])
        eq, qf = q_stage[:, 0], q_stage[:, 1]
        h1 = q_stage
        ek, kf = sb("ek", [P, 2, D]), sb("kf", [P, 2, D])
        v1 = sb("v1", [P, 2, D + 1])
        kv_sb = sb("kv_sb", [P, 2, D + 1])
        u1, x1n = sb("u1", [P, 2, TILES, D]), sb("x1n", [P, 2, TILES, D])
        h2, h3 = sb("h2", [P, 2, SEQ]), sb("h3", [P, 2, SEQ // 2])
        pq_flat = pq[:, :, :, :].rearrange("p n a d -> p (n a d)")

        def in_pq(at, n):
            return pq_flat[:, at * SEQ:(at + n) * SEQ]

        hid = [in_pq(3 * i, 3).rearrange("p (c n) -> p c n", c=CHUNKS) for i in range(2)]
        sg = [in_pq(6 + i, 1) for i in range(2)]
        u2 = [in_pq(8 + i, 1).rearrange("p (t d) -> p t d", t=TILES) for i in range(2)]
        un = [in_pq(10 + i, 1).rearrange("p (t d) -> p t d", t=TILES) for i in range(2)]
        yb = [in_pq(12 + i, 1).rearrange("p (t d) -> p t d", t=TILES) for i in range(2)]

        st = [sb(f"st{i}", [P, BATCHES, TILES, 6]) for i in range(3)]
        mv = [sb(f"mv{i}", [P, BATCHES, TILES, 2]) for i in range(3)]
        nm = [sb(f"nm{i}", [P, BATCHES, TILES]) for i in range(3)]
        ve = [sb(f"ve{i}", [P, BATCHES, TILES]) for i in range(3)]
        rstd = [sb(f"rstd{i}", [P, BATCHES, TILES]) for i in range(3)]
        nmr = [sb(f"nmr{i}", [P, BATCHES, TILES]) for i in range(3)]
        den = sb("den", [P, BATCHES, TILES])
        rden = sb("rden", [P, BATCHES, TILES])
        sum_hi, sum_lo, ctx_sum = sb("sum_hi", [P, BATCHES]), sb("sum_lo", [P, BATCHES]), sb("ctx_sum", [P, BATCHES])
        gh1, gh2, gt = sb("gh1", [P, BATCHES]), sb("gh2", [P, BATCHES]), sb("gt", [P, BATCHES])
        base = sb("base", [P, BATCHES])
        tt = sb("tt", [P, SLOTS, 2, TILES])
        cpl = sb("cpl", [P, SLOTS, 2, TILES])
        ab = sb("ab", [P, PAIRS, 6, 2 * TILES])

        bank = [ctx.enter_context(nc.psum_tensor(f"bank{i}", [P, SEQ], F32)) for i in range(6)]
        bank67 = ctx.enter_context(nc.psum_tensor("bank67", [P, TILES, SEQ // 2], F32))
        ps_xT, ps_x1T, ps_q, ps_k, ps_kv, ps_num = bank[0], bank[0], bank[2], [bank[3], bank[4], bank[1]], bank[5], bank67
        ps_h1, ps_h2 = [bank[3], bank[4]], [bank[0], bank[2]]
        ps_h3 = [bank[5][:, 0:SEQ // 2], bank67[:, 2, :]]
        ps_gf = bank[5][:, 400:400 + 3 * BATCHES].rearrange("p (a b) -> p a b", a=3)
        ps_bf = bank[5][:, 440:440 + 2 * CHUNKS]
        ps_z = bank67[:, 0, 0:SLOTS * 8].rearrange("p (s n) -> p s n", s=SLOTS)
        ps_gate, ps_up, ps_down = [bank[0], bank[1]], [bank[2], bank[3]], [bank[4], bank[5]]

        x_loaded = [sem(f"x_loaded{b}") for b in range(BATCHES)]
        first_loaded, small_loaded, ffn_loaded = sem("first_loaded"), sem("small_loaded"), sem("ffn_loaded")
        down_loaded, cols_loaded, rows_loaded = sem("down_loaded"), sem("cols_loaded"), sem("rows_loaded")
        first_ready, bias_ready, ffn_ready, bffn_ps, bffn_ready = [
            sem(n) for n in ("first_ready", "bias_ready", "ffn_ready", "bffn_ps", "bffn_ready")]
        pool_const, cols_ready, consts_ready = sem("pool_const"), sem("cols_ready"), sem("consts_ready")
        dve_step, pool_step, act_step = sem("dve_step"), sem("pool_step"), sem("act_step")
        mean_ready = [sem(f"mean_ready{i}") for i in range(3)]
        rstd_ready = [None, sem("rstd_ready1"), sem("rstd_ready2")]
        xn_ready, tx_ready = sem("xn_ready"), sem("tx_ready")
        xT_ps, xT_hi_ready, xT_lo_ready = sem("xT_ps"), sem("xT_hi_ready"), sem("xT_lo_ready")
        q_ps, eq_ready, qf_ready = sem("q_ps"), sem("eq_ready"), sem("qf_ready")
        k_ps, ek_ready, kf_ready, v_ready, pq_ready = [sem(n) for n in ("k_ps", "ek_ready", "kf_ready", "v_ready", "pq_ready")]
        kv_ps, kv_ready, num_ps, u1_ready = sem("kv_ps"), sem("kv_ready"), sem("num_ps"), sem("u1_ready")
        x1n_ready, x1T_ps, x1_hi_ready, x1_lo_ready, x1g_ready = [
            sem(n) for n in ("x1n_ready", "x1T_ps", "x1_hi_ready", "x1_lo_ready", "x1g_ready")]
        ctx_ready, gf_ps, gf_act, base_ready = sem("ctx_ready"), sem("gf_ps"), sem("gf_act"), sem("base_ready")
        h1_ps, h1_ready, h2_ps, h2_ready = sem("h1_ps"), sem("h1_ready"), sem("h2_ps"), sem("h2_ready")
        h3_ps, h3_ready, z_ps, tt_ready = sem("h3_ps"), sem("h3_ready"), sem("z_ps"), sem("tt_ready")
        r_ready, s_ready, ab_ready, ax_ready, o_ready = [
            sem(n) for n in ("r_ready", "s_ready", "ab_ready", "ax_ready", "o_ready")]
        gate_ps, up_ps, sg_ready, hid_ready = sem("gate_ps"), sem("up_ps"), sem("sg_ready"), sem("hid_ready")
        down_ps, u2_ready, un_ready = sem("down_ps"), sem("u2_ready"), sem("un_ready")
        g_ready, mn_ready, y_ready = sem("g_ready"), sem("mn_ready"), sem("y_ready")
        y_stored = [sem("y_stored0"), sem("y_stored1")]

        block = ctx.enter_context(nc.Block())

        @block.sync
        def _(sp):
            sp.dma_start(x_tok[:, 0], x_dram[0]).then_inc(x_loaded[0], 16)
            sp.dma_start(small[:], w_small).then_inc(small_loaded, 16)
            sp.dma_start(first_raw[:], w_first).then_inc(first_loaded, 16)
            sp.dma_start(x_tok[:, 1], x_dram[1]).then_inc(x_loaded[1], 16)
            sp.dma_start(row[:], rows.to_broadcast([P, row.shape[1]])).then_inc(rows_loaded, 16)
            sp.dma_start(x_tok[:, 2], x_dram[2]).then_inc(x_loaded[2], 16)
            sp.dma_start(col[:], cols).then_inc(cols_loaded, 16)
            sp.dma_start(ffn_raw[:], w_ffn).then_inc(ffn_loaded, 16)
            sp.dma_start(wd[:], w_down).then_inc(down_loaded, 16)
            for b in range(3, BATCHES):
                sp.dma_start(x_tok[:, b], x_dram[b]).then_inc(x_loaded[b], 16)
            for b in range(BATCHES):
                sp.wait_ge(y_ready, b + 1)
                sp.dma_start(out_dram[b], yb[b % 2]).then_inc(y_stored[b % 2], 16)
            for i in range(2):
                sp.wait_ge(y_stored[i], 16 * (BATCHES // 2))

        @block.gpsimd
        def _(pool):
            steps = [0]

            def link(ins):
                steps[0] += 1
                ins.then_inc(pool_step, 1)
                pool.wait_ge(pool_step, steps[0])

            def power(i, b):
                pool.wait_ge(mean_ready[i], b + 1)
                link(pool.tensor_scalar(ve[i][:, b], mv[i][:, b, :, 1], 1.0, LN_EPS, ALU.mult, ALU.add))
                return pool.tensor_tensor(rstd[i][:, b], ve[i][:, b], minus_half[:], ALU.pow)

            def norm_x(b):
                link(power(0, b))
                for t in range(TILES):
                    last = pool.tensor_scalar(xn_tok[:, b, t], x_tok[:, b, t], nm[0][:, b, t:t + 1],
                                              rstd[0][:, b, t:t + 1], ALU.add, ALU.mult)
                last.then_inc(xn_ready, 1)

            def rstd_of(i, b):
                link(power(i, b))
                pool.tensor_tensor(nmr[i][:, b], nm[i][:, b], rstd[i][:, b], ALU.mult).then_inc(rstd_ready[i], 1)

            def scale_x1(b):
                pool.wait_ge(x1n_ready, b + 1)
                if b == 0:
                    pool.wait_ge(rows_loaded, 16)
                pool.tensor_tensor(x1g[:, b], x1n[:, b % 2], row_g1.unsqueeze(1).to_broadcast([P, TILES, D]),
                                   ALU.mult).then_inc(x1g_ready, 1)

            def twist_x(b):
                pool.wait_ge(xn_ready, b + 1)
                for to, frm, s in ((0, 2, 1.0), (1, 3, -1.0), (2, 0, -1.0), (3, 1, 1.0)):
                    last = pool.tensor_scalar(tx_tok[:, b, :, to * BLK:(to + 1) * BLK],
                                              xn_tok[:, b, :, frm * BLK:(frm + 1) * BLK], s, 0.0, ALU.mult, ALU.add)
                last.then_inc(tx_ready, 1)

            def s_pair(j):
                pool.wait_ge(r_ready, j + 1)
                n0, n1 = 8 * j, 8 * j + 8
                c0 = cpl[:, j].rearrange("p a t -> p (a t)").unsqueeze(2).to_broadcast([P, 8, D])
                link(pool.tensor_tensor(pq[:, n0:n1, 0], pq[:, n0:n1, 0], c0, ALU.mult))
                pool.tensor_tensor(pq[:, n0:n1, 1], pq[:, n0:n1, 1], pq[:, n0:n1, 0],
                                   ALU.subtract).then_inc(s_ready, 1)

            def ax_pair(j):
                pool.wait_ge(ab_ready, j + 1)
                pool.wait_ge(tx_ready, 2 * j + 2)
                for b in (2 * j, 2 * j + 1):
                    a = ab[:, j, 2, TILES * (b % 2):TILES * (b % 2) + TILES].unsqueeze(2).to_broadcast([P, TILES, D])
                    pool.tensor_tensor(xn_tok[:, b], xn_tok[:, b], a, ALU.mult).then_inc(ax_ready, 1)

            def gate_rows(b):
                pool.wait_ge(g_ready, b + 1)
                pool.tensor_tensor(tx_tok[:, b], xn_tok[:, b], row_g2.unsqueeze(1).to_broadcast([P, TILES, D]),
                                   ALU.mult)
                link(pool.tensor_tensor(xn_tok[:, b], xn_tok[:, b],
                                        row_b2.unsqueeze(1).to_broadcast([P, TILES, D]), ALU.mult))
                pool.tensor_tensor(x_tok[:, b], x_tok[:, b], xn_tok[:, b], ALU.add).then_inc(mn_ready, 1)

            pool.memset(minus_half[:], -0.5).then_inc(pool_const, 1)
            pool.wait_ge(pool_const, 1)
            norm_x(0)
            norm_x(1)
            for b in range(BATCHES + 2):
                if b + 2 < BATCHES:
                    norm_x(b + 2)
                if 1 <= b <= BATCHES:
                    rstd_of(1, b - 1)
                if b < BATCHES:
                    twist_x(b)
                if 2 <= b:
                    scale_x1(b - 2)
            for j in range(PAIRS):
                s_pair(j)
            for j in range(PAIRS):
                ax_pair(j)
            for b in range(BATCHES + 1):
                if b < BATCHES:
                    gate_rows(b)
                if b >= 1:
                    rstd_of(2, b - 1)

        @block.scalar
        def _(act):
            def hi_x(b):
                act.wait_ge(xT_ps, b + 1)
                if b >= 2:
                    act.wait_ge(k_ps, TILES * (b - 1))
                act.activation(xT_hi[:, b % 2], ps_xT[:], ACT.Identity,
                               accum_out=sum_hi[:, b:b + 1]).then_inc(xT_hi_ready, 1)

            def exp_q(b):
                act.wait_ge(q_ps, b + 1)
                if b >= 2:
                    act.wait_ge(qf_ready, b - 1)
                act.activation(eq[:, b % 2], ps_q[:], ACT.Exp, bias=minus_one[:, 0:1]).then_inc(eq_ready, 1)

            def token_tile(n):
                act.wait_ge(k_ps, n + 1)
                if n >= 2:
                    act.wait_ge(kf_ready, n - 1)
                act.activation(ek[:, n % 2], ps_k[n % 3][:, 0:D], ACT.Exp, bias=minus_one[:, 0:1]).then_inc(ek_ready, 1)
                if n >= 2:
                    act.wait_ge(kv_ps, n - 1)
                act.copy(v1[:, n % 2, 0:D], ps_k[n % 3][:, D:2 * D]).then_inc(v_ready, 1)
                act.copy(pq[:, n].rearrange("p a d -> p (a d)"), ps_k[n % 3][:, 2 * D:4 * D]).then_inc(pq_ready, 1)

            def norm_1(b):
                act.wait_ge(rstd_ready[1], b + 1)
                if b >= 2:
                    act.wait_ge(x1T_ps, b - 1)
                    act.wait_ge(x1g_ready, b - 1)
                for t in range(TILES):
                    last = act.activation(x1n[:, b % 2, t], u1[:, b % 2, t], ACT.Identity,
                                          scale=rstd[1][:, b, t:t + 1], bias=nmr[1][:, b, t:t + 1])
                last.then_inc(x1n_ready, 1)

            def hi_x1(b):
                act.wait_ge(x1T_ps, b + 1)
                act.copy(x1_hi[:, b], ps_x1T[:]).then_inc(x1_hi_ready, 1)

            def gelu_1(s):
                for par in range(2):
                    m = 2 * s + par
                    act.wait_ge(h1_ps, m + 1)
                    if s >= 2:
                        act.wait_ge(h2_ps, s - 1)
                    act.activation(h1[:, s % 2, par], ps_h1[par][:], ACT.Gelu,
                                   bias=col[:, COL["cn_b1"]:COL["cn_b1"] + 1]).then_inc(h1_ready, 1)

            def gelu_2(s):
                act.wait_ge(h2_ps, s + 1)
                if s >= 2:
                    act.wait_ge(h3_ps, s - 1)
                act.activation(h2[:, s % 2], ps_h2[s % 2][:], ACT.Gelu,
                               bias=col[:, COL["cn_b2"]:COL["cn_b2"] + 1]).then_inc(h2_ready, 1)

            def gelu_3(s):
                act.wait_ge(h3_ps, s + 1)
                if s >= 2:
                    act.wait_ge(z_ps, s - 1)
                act.activation(h3[:, s % 2], ps_h3[s % 2], ACT.Gelu,
                               bias=col[:, COL["cn_b3"]:COL["cn_b3"] + 1]).then_inc(h3_ready, 1)

            def tanh_z(s):
                act.wait_ge(z_ps, s + 1)
                act.activation(tt[:, s].rearrange("p par (ch u) -> p u ch par", ch=2),
                               ps_z[:, s].rearrange("p (u ch par) -> p u ch par", u=2, ch=2), ACT.Tanh,
                               bias=half_b4[:, 0:1], scale=0.5).then_inc(tt_ready, 1)

            def silu_o(b):
                act.wait_ge(o_ready, b + 1)
                act.activation(xn_tok[:, b], xn_tok[:, b], ACT.Silu).then_inc(g_ready, 1)

            def silu_gate(n):
                b, c = divmod(n, CHUNKS)
                act.wait_ge(gate_ps, n + 1)
                if n >= 2:
                    act.wait_ge(hid_ready, n - 1)
                if n == 0:
                    act.wait_ge(bffn_ready, 1)
                m = CHUNK_ROWS[c]
                act.activation(sg[n % 2][0:m], ps_gate[n % 2][0:m], ACT.Silu,
                               bias=bffn[0:m, c:c + 1]).then_inc(sg_ready, 1)

            def norm_2(b):
                act.wait_ge(rstd_ready[2], b + 1)
                if b >= 2:
                    act.wait_ge(y_ready, b - 1)
                for t in range(TILES):
                    last = act.activation(un[b % 2][:, t], u2[b % 2][:, t], ACT.Identity,
                                          scale=rstd[2][:, b, t:t + 1], bias=nmr[2][:, b, t:t + 1])
                last.then_inc(un_ready, 1)

            act.wait_ge(consts_ready, 1)
            hi_x(0)
            for b in range(BATCHES + 1):
                if b + 1 < BATCHES:
                    hi_x(b + 1)
                if b < BATCHES:
                    exp_q(b)
                    for t in range(TILES):
                        token_tile(TILES * b + t)
                if 2 <= b:
                    hi_x1(b - 2)
                if b >= 1:
                    norm_1(b - 1)
            act.wait_ge(cols_ready, 1)
            act.wait_ge(gf_ps, 1)
            act.activation(gh1[0:64], ps_gf[0:64, 0], ACT.Gelu, scale=1.0 / SEQ,
                           bias=col[0:64, COL["gc_b1"]:COL["gc_b1"] + 1]).then_inc(gf_act, 1)
            act.wait_ge(gf_ps, 2)
            act.activation(gh2[0:32], ps_gf[0:32, 1], ACT.Gelu,
                           bias=col[0:32, COL["gc_b2"]:COL["gc_b2"] + 1]).then_inc(gf_act, 1)
            act.wait_ge(gf_ps, 3)
            act.activation(gt[:], ps_gf[:, 2], ACT.Tanh, scale=0.5, bias=half_gb3[:, 0:1]).then_inc(gf_act, 1)
            for s in range(SLOTS + 2):
                if s < SLOTS:
                    gelu_1(s)
                if s == 0:
                    hi_x1(BATCHES - 1)
                if 1 <= s <= SLOTS:
                    gelu_3(s - 1)
                if s >= 2:
                    tanh_z(s - 2)
                if s < SLOTS:
                    gelu_2(s)
            for b in range(BATCHES + 2):
                if b < BATCHES:
                    for c in range(CHUNKS):
                        silu_gate(CHUNKS * b + c)
                    silu_o(b)
                if 2 <= b:
                    norm_2(b - 2)

        @block.vector
        def _(dve):
            steps = [0]

            def mark(ins):
                steps[0] += 1
                ins.then_inc(dve_step, 1)
                return ins

            def link(ins):
                mark(ins)
                dve.wait_ge(dve_step, steps[0])

            def stats(i, b, src):
                for t in range(TILES):
                    last = dve.bn_stats(st[i][:, b, t], src[:, t])
                link(last)
                for t in range(TILES):
                    last = dve.bn_aggr(mv[i][:, b, t], st[i][:, b, t])
                link(last)
                dve.tensor_scalar(nm[i][:, b], mv[i][:, b, :, 0], -1.0, None, ALU.mult).then_inc(mean_ready[i], 1)

            def stats_x(b):
                dve.wait_ge(x_loaded[b], 16)
                stats(0, b, x_tok[:, b])

            def lo_x(b):
                dve.wait_ge(xT_hi_ready, b + 1)
                if b >= 2:
                    dve.wait_ge(k_ps, TILES * (b - 1))
                dve.scalar_tensor_tensor(out=xT_lo[:, b % 2], in0=ps_xT[:], scalar=1.0,
                                         in1=xT_hi[:, b % 2].bitcast(F32), op0=ALU.mult, op1=ALU.subtract,
                                         accum_out=sum_lo[:, b:b + 1]).then_inc(xT_lo_ready, 1)

            def feature_q(b):
                dve.wait_ge(eq_ready, b + 1)
                if b >= 2:
                    dve.wait_ge(num_ps, b - 1)
                dve.scalar_tensor_tensor(out=qf[:, b % 2], in0=eq[:, b % 2], scalar=1.0, in1=ps_q[:],
                                         op0=ALU.min, op1=ALU.max).then_inc(qf_ready, 1)

            def feature_k(n):
                dve.wait_ge(pq_ready, n + 1)
                if n >= 2:
                    dve.wait_ge(kv_ps, n - 1)
                dve.scalar_tensor_tensor(out=kf[:, n % 2], in0=ek[:, n % 2], scalar=1.0, in1=ps_k[n % 3][:, 0:D],
                                         op0=ALU.min, op1=ALU.max).then_inc(kf_ready, 1)

            def copy_kv(b):
                dve.wait_ge(kv_ps, TILES * (b + 1))
                if b >= 2:
                    dve.wait_ge(num_ps, b - 1)
                dve.tensor_copy(kv_sb[:, b % 2], ps_kv[:, 0:D + 1]).then_inc(kv_ready, 1)

            def attend(b):
                dve.wait_ge(num_ps, b + 1)
                link(dve.tensor_scalar(den[:, b], ps_num[:, :, D], ATTN_EPS, None, ALU.add))
                link(dve.reciprocal(rden[:, b], den[:, b]))
                if b >= 2:
                    dve.wait_ge(x1n_ready, b - 1)
                for t in range(TILES):
                    last = dve.scalar_tensor_tensor(out=u1[:, b % 2, t], in0=ps_num[:, t, 0:D],
                                                    scalar=rden[:, b, t:t + 1], in1=xn_tok[:, b, t],
                                                    op0=ALU.mult, op1=ALU.add)
                last.then_inc(u1_ready, 1)
                dve.wait_ge(u1_ready, b + 1)
                stats(1, b, u1[:, b % 2])

            def lo_x1(b):
                dve.wait_ge(x1_hi_ready, b + 1)
                dve.tensor_tensor(x1_lo[:, b], ps_x1T[:], x1_hi[:, b].bitcast(F32), ALU.subtract).then_inc(x1_lo_ready, 1)

            def coupling(s):
                j = s % PAIRS
                dve.wait_ge(tt_ready, s + 1)
                if s == 0:
                    dve.wait_ge(base_ready, 1)
                link(dve.scalar_tensor_tensor(out=cpl[:, s], in0=tt[:, s], scalar=gain[:, 1:2],
                                              in1=base[:, 2 * j:2 * j + 2].unsqueeze(2).to_broadcast([P, 2, TILES]),
                                              op0=ALU.mult, op1=ALU.add))

            def next_r(s):
                cycle, j = divmod(s, PAIRS)
                if cycle == 1:
                    dve.wait_ge(s_ready, j + 1)
                for i in range(2 * TILES):
                    n = 2 * TILES * j + i
                    last = dve.scalar_tensor_tensor(out=r_tok[:, n], in0=pq[:, n, 1],
                                                    scalar=cpl[:, s, i // TILES, i % TILES:i % TILES + 1],
                                                    in1=pq[:, n, 0] if cycle == 0 else r_tok[:, n],
                                                    op0=ALU.mult, op1=ALU.add)
                last.then_inc(r_ready, 1)

            def scalars_ab(j):
                c0, c1, c2 = [cpl[:, j + PAIRS * n].rearrange("p a t -> p (a t)") for n in range(CYCLES)]
                a1, b1, a, b, t0, t1 = [ab[:, j, i] for i in (0, 1, 2, 3, 4, 5)]
                dve.tensor_tensor(t0, c0, c1, ALU.mult)
                link(dve.tensor_tensor(b1, c0, c1, ALU.add))
                dve.tensor_scalar(a1, t0, -1.0, 1.0, ALU.mult, ALU.add)
                link(dve.tensor_tensor(t1, c2, b1, ALU.mult))
                dve.tensor_tensor(a, a1, t1, ALU.subtract)
                link(dve.tensor_tensor(t0, c2, a1, ALU.mult))
                dve.tensor_tensor(b, b1, t0, ALU.add).then_inc(ab_ready, 1)

            def o3(b):
                j = b // 2
                dve.wait_ge(ax_ready, b + 1)
                for t in range(TILES):
                    i = TILES * (b % 2) + t
                    last = dve.scalar_tensor_tensor(out=xn_tok[:, b, t], in0=tx_tok[:, b, t],
                                                    scalar=ab[:, j, 3, i:i + 1], in1=xn_tok[:, b, t],
                                                    op0=ALU.mult, op1=ALU.add)
                last.then_inc(o_ready, 1)

            def hidden(n):
                b, c = divmod(n, CHUNKS)
                m = CHUNK_ROWS[c]
                dve.wait_ge(up_ps, n + 1)
                dve.wait_ge(sg_ready, n + 1)
                if b >= 2:
                    dve.wait_ge(down_ps, b - 1)
                dve.scalar_tensor_tensor(out=hid[b % 2][0:m, c], in0=ps_up[n % 2][0:m],
                                         scalar=bffn[0:m, CHUNKS + c:CHUNKS + c + 1], in1=sg[n % 2][0:m],
                                         op0=ALU.add, op1=ALU.mult).then_inc(hid_ready, 1)

            def residual_2(b):
                dve.wait_ge(down_ps, b + 1)
                dve.wait_ge(x1g_ready, b + 1)
                if b >= 2:
                    dve.wait_ge(un_ready, b - 1)
                dve.tensor_tensor(u2[b % 2], ps_down[b % 2][:].rearrange("p (t d) -> p t d", t=TILES), x1g[:, b],
                                  ALU.add).then_inc(u2_ready, 1)
                dve.wait_ge(u2_ready, b + 1)
                stats(2, b, u2[b % 2])

            def finish(b):
                dve.wait_ge(un_ready, b + 1)
                dve.wait_ge(mn_ready, b + 1)
                if b >= 2:
                    dve.wait_ge(y_stored[b % 2], 16 * (b // 2))
                link(dve.tensor_tensor(yb[b % 2], un[b % 2], tx_tok[:, b], ALU.mult))
                dve.tensor_tensor(yb[b % 2], yb[b % 2], x_tok[:, b], ALU.add).then_inc(y_ready, 1)

            def split_bias():
                for at in (0, 32, 64):
                    link(dve.tensor_copy(bias_b[:], bias_rest[:]))
                    if at < 64:
                        link(dve.tensor_tensor(bias_rest[:], bias_rest[:], bias_b[:], ALU.subtract))
                    if at < 64:
                        link(dve.tensor_copy(bias3[at:at + 1], bias_b[at:at + 1]))
                    else:
                        dve.tensor_copy(bias3[at:at + 1], bias_b[at:at + 1]).then_inc(bias_ready, 1)

            dve.memset(minus_one[:], -1.0)
            dve.memset(bias3[:], 0.0)
            dve.memset(ones_bf[:], 1.0)
            dve.memset(v1[:, :, D:D + 1], 1.0)
            for i, s in enumerate((-1.0, 1.0, 1.0, -1.0)):
                last = dve.memset(sign[BLK * i:BLK * (i + 1)], s)
            last.then_inc(consts_ready, 1)
            dve.wait_ge(consts_ready, 1)
            stats_x(0)
            dve.wait_ge(first_loaded, 16)
            link(dve.tensor_scalar(first_raw[:, 3 * D:4 * D], first_raw[:, 3 * D:4 * D], sign[:, 0:1], None, ALU.mult))
            link(dve.tensor_copy(first_hi[:], first_raw[:]))
            dve.tensor_tensor(first_lo[:], first_raw[:], first_hi[:].bitcast(F32), ALU.subtract).then_inc(first_ready, 1)
            stats_x(1)
            dve.wait_ge(rows_loaded, 16)
            dve.tensor_scalar(bias_rest[:, 0:2 * D], row_bqkv[:, 0:2 * D], 1.0, None, ALU.add)
            dve.tensor_copy(bias_rest[:, 2 * D:3 * D], row_bqkv[:, 2 * D:3 * D])
            link(dve.tensor_tensor(bias_rest[:, 3 * D:4 * D], row_bd, row_b1, ALU.add))
            split_bias()
            lo_x(0)
            dve.wait_ge(cols_loaded, 16)
            dve.tensor_scalar(half_b4[:], col[:, COL["cn_b4"]:COL["cn_b4"] + 1], 0.5, None, ALU.mult)
            dve.tensor_scalar(half_gb3[:], col[:, COL["gc_b3"]:COL["gc_b3"] + 1], 0.5, None, ALU.mult)
            dve.tensor_scalar(gain[:, 0:1], col[:, COL["range"]:COL["range"] + 1], W_GLOBAL, None, ALU.mult)
            dve.tensor_scalar(gain[:, 1:2], col[:, COL["range"]:COL["range"] + 1], W_TOKEN, None,
                              ALU.mult).then_inc(cols_ready, 1)

            for b in range(BATCHES + 2):
                if b + 2 < BATCHES:
                    stats_x(b + 2)
                if b + 1 < BATCHES:
                    lo_x(b + 1)
                if b < BATCHES:
                    feature_q(b)
                    for t in range(TILES):
                        feature_k(TILES * b + t)
                    copy_kv(b)
                if 1 <= b <= BATCHES:
                    attend(b - 1)
                if b == 1:
                    dve.wait_ge(ffn_loaded, 16)
                    link(dve.tensor_scalar(ffn_scaled[:], ffn_raw[:], col[:, COL["g1"]:COL["g1"] + 1], None, ALU.mult))
                    link(dve.tensor_copy(ffn_hi[:], ffn_scaled[:]))
                    dve.tensor_tensor(ffn_lo[:], ffn_scaled[:], ffn_hi[:].bitcast(F32),
                                      ALU.subtract).then_inc(ffn_ready, 1)
                if b == BATCHES:
                    dve.wait_ge(xT_hi_ready, BATCHES)
                    dve.wait_ge(xT_lo_ready, BATCHES)
                    dve.tensor_tensor(ctx_sum[:], sum_hi[:], sum_lo[:], ALU.add).then_inc(ctx_ready, 1)
                if 2 <= b:
                    lo_x1(b - 2)
                if b == BATCHES:
                    dve.wait_ge(bffn_ps, 1)
                    for c, m in enumerate(CHUNK_ROWS):
                        last = dve.tensor_tensor(bffn[0:m, c::CHUNKS], ps_bf[0:m, c::CHUNKS],
                                                 col[0:m, COL["bg0"] + c::CHUNKS], ALU.add)
                    last.then_inc(bffn_ready, 1)
            dve.wait_ge(gf_act, 3)
            dve.tensor_scalar(base[:], gt[:], gain[:, 0:1], BASE_COUPLING, ALU.mult, ALU.add).then_inc(base_ready, 1)
            for s in range(SLOTS):
                coupling(s)
                if s < 2 * PAIRS:
                    next_r(s)
                else:
                    scalars_ab(s - 2 * PAIRS)
            for b in range(2):
                o3(b)
            for b in range(BATCHES + 2):
                if b < BATCHES:
                    for c in range(CHUNKS):
                        hidden(CHUNKS * b + c)
                if 1 <= b <= BATCHES:
                    residual_2(b - 1)
                if b + 2 < BATCHES:
                    o3(b + 2)
                if b >= 2:
                    finish(b - 2)

        @block.tensor
        def _(pe):
            def transposes(dst, src):
                for t in range(TILES):
                    last = pe.transpose(dst[:, t * P:(t + 1) * P], src[:, t], eye)
                return last

            def transpose_x(b):
                pe.wait_ge(xn_ready, b + 1)
                if b >= 1:
                    pe.wait_ge(xT_lo_ready, b)
                if b >= 4:
                    pe.wait_ge(x1_lo_ready, b - 3)
                transposes(ps_xT, xn_tok[:, b]).then_inc(xT_ps, 1)

            def project_q(b):
                pe.wait_ge(xT_lo_ready, b + 1)
                if b == 0:
                    pe.wait_ge(first_ready, 1)
                    pe.wait_ge(bias_ready, 1)
                if b >= 1:
                    pe.wait_ge(qf_ready, b)
                hi, lo = xT_hi[:, b % 2], xT_lo[:, b % 2]
                wq = slice(4 * D, 5 * D)
                pe.matmul(ps_q[:], first_hi[:, wq], hi, start=True, stop=False)
                pe.matmul(ps_q[:], first_hi[:, wq], lo, start=False, stop=False)
                pe.matmul(ps_q[:], first_lo[:, wq], hi, start=False, stop=False)
                pe.matmul(ps_q[:], bias3[:, 0:D], ones_bf[:], start=False, stop=True).then_inc(q_ps, 1)

            def project_tokens(n):
                b, t = divmod(n, TILES)
                if n >= 3:
                    pe.wait_ge(kf_ready, n - 2)
                dst = ps_k[n % 3]
                hi, lo = xT_hi[:, b % 2, t * P:(t + 1) * P], xT_lo[:, b % 2, t * P:(t + 1) * P]
                pe.matmul(dst[:], hi, first_hi[:, 0:4 * D], start=True, stop=False)
                pe.matmul(dst[:], hi, first_lo[:, 0:4 * D], start=False, stop=False)
                pe.matmul(dst[:, 0:2 * D], ones_bf[:, 0:P], bias3[:, D:3 * D], start=False, stop=False)
                pe.matmul(dst[:], lo, first_hi[:, 0:4 * D], start=False, stop=True).then_inc(k_ps, 1)

            def sum_kv(n):
                b, t = divmod(n, TILES)
                pe.wait_ge(kf_ready, n + 1)
                pe.wait_ge(v_ready, n + 1)
                if t == 0 and b >= 1:
                    pe.wait_ge(kv_ready, b)
                pe.matmul(ps_kv[:, 0:D + 1], kf[:, n % 2], v1[:, n % 2], start=(t == 0),
                          stop=(t == TILES - 1)).then_inc(kv_ps, 1)

            def numerator(b):
                pe.wait_ge(kv_ready, b + 1)
                pe.wait_ge(qf_ready, b + 1)
                if b >= 1:
                    pe.wait_ge(u1_ready, b)
                for t in range(TILES):
                    last = pe.matmul(ps_num[:, t, 0:D + 1], qf[:, b % 2, t * P:(t + 1) * P], kv_sb[:, b % 2],
                                     start=True, stop=True)
                last.then_inc(num_ps, 1)

            def transpose_x1(b):
                pe.wait_ge(x1n_ready, b + 1)
                if b >= 1:
                    pe.wait_ge(x1_lo_ready, b)
                pe.wait_ge(xT_lo_ready, min(b + 4, BATCHES))
                transposes(ps_x1T, x1n[:, b % 2]).then_inc(x1T_ps, 1)

            def layer_1(s):
                cycle, j = divmod(s, PAIRS)
                if cycle >= 1:
                    pe.wait_ge(r_ready, s - PAIRS + 1)
                for par in range(2):
                    m = 2 * s + par
                    if m >= 2:
                        pe.wait_ge(h1_ready, m - 1)
                    n0 = 2 * TILES * j + TILES * par
                    src = pq[:, n0:n0 + TILES, 0] if cycle == 0 else r_tok[:, n0:n0 + TILES]
                    transposes(ps_h1[par], src).then_inc(h1_ps, 1)

            def layer_2(s):
                pe.wait_ge(h1_ready, 2 * s + 2)
                if s >= 2:
                    pe.wait_ge(h2_ready, s - 1)
                for par in range(2):
                    last = pe.matmul(ps_h2[s % 2][64 * par:64 * par + 64, :], sm("cn_w2"), h1[:, s % 2, par],
                                     start=True, stop=True)
                last.then_inc(h2_ps, 1)

            def layer_3(s):
                pe.wait_ge(h2_ready, s + 1)
                if s >= 2:
                    pe.wait_ge(h3_ready, s - 1)
                for ch in range(2):
                    last = pe.matmul(ps_h3[s % 2][64 * ch:64 * ch + 64, :], sm("cn_w3"),
                                     h2[:, s % 2, ch * 256:(ch + 1) * 256], start=True, stop=True)
                last.then_inc(h3_ps, 1)

            def layer_4(s):
                pe.wait_ge(h3_ready, s + 1)
                if s >= 1:
                    pe.wait_ge(tt_ready, s)
                for u in range(2):
                    last = pe.matmul(ps_z[:, s, 4 * u:4 * u + 4], h3[:, s % 2, u * P:(u + 1) * P], sm("cn_w4"),
                                     start=True, stop=True)
                last.then_inc(z_ps, 1)

            def gate_up(n):
                b, c = divmod(n, CHUNKS)
                m = CHUNK_ROWS[c]
                if n >= 2:
                    pe.wait_ge(sg_ready, n - 1)
                for k, (dst, done) in enumerate(((ps_gate, gate_ps), (ps_up, up_ps))):
                    if k == 1 and n >= 2:
                        pe.wait_ge(hid_ready, n - 1)
                    w = slice(k * HID + c * P, k * HID + c * P + m)
                    pe.matmul(dst[n % 2][0:m], ffn_hi[:, w], x1_hi[:, b], start=True, stop=False)
                    pe.matmul(dst[n % 2][0:m], ffn_hi[:, w], x1_lo[:, b], start=False, stop=False)
                    pe.matmul(dst[n % 2][0:m], ffn_lo[:, w], x1_hi[:, b], start=False, stop=True).then_inc(done, 1)

            def down(b):
                pe.wait_ge(hid_ready, CHUNKS * (b + 1))
                if b >= 2:
                    pe.wait_ge(u2_ready, b - 1)
                dst = ps_down[b % 2]
                for t in range(TILES):
                    pe.matmul(dst[:, t * P:(t + 1) * P], ones_bf[:, 0:P], bias3[:, 3 * D:4 * D], start=True, stop=False)
                    for c, m in enumerate(CHUNK_ROWS):
                        last = pe.matmul(dst[:, t * P:(t + 1) * P], hid[b % 2][0:m, c, t * P:(t + 1) * P],
                                         wd[0:m, c], start=False, stop=(c == CHUNKS - 1))
                last.then_inc(down_ps, 1)

            pe.wait_ge(small_loaded, 16)
            transpose_x(0)
            for b in range(BATCHES):
                if b + 1 < BATCHES:
                    transpose_x(b + 1)
                project_q(b)
                for t in range(TILES):
                    project_tokens(TILES * b + t)
                    if t >= 1:
                        sum_kv(TILES * b + t - 1)
                    if t == 1 and b >= 1:
                        numerator(b - 1)
                    if t == 3 and b >= 2:
                        transpose_x1(b - 2)
                sum_kv(TILES * b + TILES - 1)
            pe.wait_ge(kv_ready, BATCHES)
            pe.wait_ge(ffn_loaded, 16)
            pe.wait_ge(cols_loaded, 16)
            for i in range(2 * CHUNKS):
                k, c = divmod(i, CHUNKS)
                m = CHUNK_ROWS[c]
                last = pe.matmul(ps_bf[0:m, i:i + 1], ffn_raw[:, k * HID + c * P:k * HID + c * P + m],
                                 col[:, COL["b1"]:COL["b1"] + 1], start=True, stop=True)
            last.then_inc(bffn_ps, 1)
            numerator(BATCHES - 1)
            transpose_x1(BATCHES - 2)
            pe.wait_ge(ctx_ready, 1)
            pe.wait_ge(bffn_ready, 1)
            pe.matmul(ps_gf[0:64, 0], sm("gc_w1"), ctx_sum[:], start=True, stop=True).then_inc(gf_ps, 1)
            pe.wait_ge(gf_act, 1)
            pe.matmul(ps_gf[0:32, 1], sm("gc_w2", 64), gh1[0:64], start=True, stop=True).then_inc(gf_ps, 1)
            pe.wait_ge(gf_act, 2)
            pe.matmul(ps_gf[:, 2], sm("gc_w3", 32), gh2[0:32], start=True, stop=True).then_inc(gf_ps, 1)
            pe.wait_ge(kf_ready, NTILE)
            pe.wait_ge(pq_ready, NTILE)
            for s in range(SLOTS + 2):
                if s < SLOTS:
                    layer_1(s)
                if s == 0:
                    pe.wait_ge(u1_ready, BATCHES)
                    pe.wait_ge(gf_act, 3)
                if s == 0:
                    transpose_x1(BATCHES - 1)
                    pe.wait_ge(x1_lo_ready, BATCHES)
                if 1 <= s <= SLOTS:
                    layer_3(s - 1)
                if s >= 2:
                    layer_4(s - 2)
                if s < SLOTS:
                    layer_2(s)
            pe.wait_ge(h1_ready, 2 * SLOTS)
            pe.wait_ge(h2_ready, SLOTS)
            pe.wait_ge(h3_ready, SLOTS)
            pe.wait_ge(ffn_ready, 1)
            pe.wait_ge(x1_lo_ready, BATCHES)
            pe.wait_ge(down_loaded, 16)
            pe.wait_ge(bffn_ready, 1)
            for b in range(BATCHES + 1):
                if b < BATCHES:
                    for c in range(CHUNKS):
                        gate_up(CHUNKS * b + c)
                if b >= 1:
                    down(b - 1)


def kernel(**inputs):
    import numpy as np
    import concourse.bacc as bacc
    from concourse.bass_utils import run_bass_kernel_spmd

    a = {k: np.asarray(v) for k, v in inputs.items()}
    w = {k.split("_", 2)[2]: v for k, v in a.items() if k.startswith("L0_ffn")}
    t = {k.split("_", 2)[2]: v for k, v in a.items() if k.startswith("L0_attn")}
    f32 = np.float32

    def padded(v, rows, at=0):
        out = np.zeros((rows,) + v.shape[1:], f32)
        out[at:at + v.shape[0]] = v
        return out

    wqkv = t["Wqkv"]
    w_first = np.concatenate([wqkv[:, D:3 * D], w["cn_w1"],
                              np.concatenate([w["cn_w1"][2 * BLK:], w["cn_w1"][:2 * BLK]]), wqkv[:, 0:D]], axis=1)
    w3 = np.zeros((P, 64), f32)
    w4 = np.zeros((P, 4), f32)
    for i in range(2):
        w3[64 * i:64 * i + 64, 32 * i:32 * i + 32] = w["cn_w3"]
    for i in range(4):
        w4[32 * i:32 * i + 32, i:i + 1] = w["cn_w4"]
    w_small = np.concatenate([w["cn_w2"], w3, w4, w["gc_w1"], padded(w["gc_w2"], P),
                              padded(np.repeat(w["gc_w3"], P, axis=1), P), np.eye(P, dtype=f32)], axis=1)
    w_ffn = np.concatenate([t["Wg"], t["Wu"]], axis=1)
    w_down = padded(t["Wd"], CHUNKS * P).reshape(CHUNKS, P, D).transpose(1, 0, 2)
    cols = [w["cn_b1"], np.tile(w["cn_b2"], 2), np.tile(w["cn_b3"], 4), np.repeat(w["cn_b4"], P),
            np.repeat(w["adaptive_range"], P), padded(w["gc_b1"], P), padded(w["gc_b2"], P),
            np.repeat(w["gc_b3"], P), t["g1"], t["b1"]]
    for name in ("bg", "bu"):
        cols += list(padded(t[name], CHUNKS * P).reshape(CHUNKS, P))
    rows = np.concatenate([t["bqkv"], t["bd"], t["b1"], t["g1"], t["g2"], t["b2"]])[None]
    sent = {"x": t["x"], "w_first": w_first, "w_small": w_small, "w_ffn": w_ffn, "w_down": w_down,
            "cols": np.stack(cols, axis=1), "rows": rows}

    nc = bacc.Bacc("TRN2", target_bir_lowering=False, num_devices=1)
    arrays, args = {}, []
    for name, v in sent.items():
        v = np.ascontiguousarray(v)
        arrays[f"in_{name}"] = v
        args.append(nc.dram_tensor(f"in_{name}", v.shape, mybir.dt.from_np(v.dtype), kind="ExternalInput").ap())
    out = nc.dram_tensor("out", sent["x"].shape, F32, kind="ExternalOutput").ap()
    gated_block(nc, *args, out)
    result = run_bass_kernel_spmd(nc, [arrays], core_ids=[0])
    return result.results[0]["out"]
```

```python
from contextlib import ExitStack

import concourse.bass as bass
from concourse import mybir

F32 = mybir.dt.float32
F32R = mybir.dt.float32r
BF16 = mybir.dt.bfloat16
ALU = mybir.AluOpType
ACT = mybir.ActivationFunctionType

P = 128
BATCHES, SEQ, D = 8, 512, 128
TILES = SEQ // P
NTILE = BATCHES * TILES
HID = 2 * 512 // 3
CHUNKS = -(-HID // P)
CHUNK_ROWS = [min(P, HID - c * P) for c in range(CHUNKS)]
S_TILES = 6
PAIRS = BATCHES // 2
CYCLES = 3
SLOTS = CYCLES * PAIRS
LN_EPS, ATTN_EPS = 1e-5, 1e-6
BASE_COUPLING, W_GLOBAL, W_TOKEN = 0.1, 0.7, 0.3
BLK = D // 4

COLS = ["bq", "bk", "bv", "bd", "cn_b1", "cn_b2", "cn_b3", "cn_b4", "range", "gc_b1", "gc_b2", "gc_b3", "g1", "b1"] + \
    [f"bg{c}" for c in range(CHUNKS)] + [f"bu{c}" for c in range(CHUNKS)]
COL = {name: i for i, name in enumerate(COLS)}
SMALL = {"cn_w2": 64, "cn_w3": 64, "cn_w4": 4, "gc_w1": 64, "gc_w2": 32, "gc_w3": P, "eye": P}
SMALL_AT = {n: sum(list(SMALL.values())[:i]) for i, n in enumerate(SMALL)}


def gated_block(nc, x, w_first, w_small, w_ffn, w_down, cols, rows, out):
    x_dram = x.rearrange("b (p t) d -> b p (t d)", t=TILES)
    out_dram = out.rearrange("b (p t) d -> b p (t d)", t=TILES)

    with ExitStack() as ctx:
        def sb(name, shape, dt=F32):
            return ctx.enter_context(nc.sbuf_tensor(name, shape, dt))

        def sem(name):
            return ctx.enter_context(nc.semaphore(name))

        first_hi, first_lo = sb("first_hi", [P, 640], F32R), sb("first_lo", [P, 640], F32R)
        small = sb("small", [P, sum(SMALL.values())])
        ffn_hi, ffn_lo = sb("ffn_hi", [P, 2 * HID], F32R), sb("ffn_lo", [P, 2 * HID], F32R)
        wd = sb("wd", [P, CHUNKS, D])
        col = sb("col", [P, len(COLS)])
        row = sb("row", [P, 3 * D])
        bias3 = sb("bias3", [P, 384 + D], BF16)
        bias_col = sb("bias_col", [P, 4])
        bias_split = sb("bias_split", [P, 4, 4], BF16)
        eye_bf = sb("eye_bf", [P, P], BF16)
        ones_bf = sb("ones_bf", [P, SEQ], BF16)
        sign = sb("sign", [P, 1])
        minus_one = sb("minus_one", [P, 1])
        minus_half = sb("minus_half", [P, TILES])
        half_b4 = sb("half_b4", [P, 1])
        half_gb3 = sb("half_gb3", [P, 1])
        gain = sb("gain", [P, 2])
        bffn = sb("bffn", [P, 2 * CHUNKS])

        eye = small[:, SMALL_AT["eye"]:SMALL_AT["eye"] + P]

        def sm(name, rows_=P):
            return small[0:rows_, SMALL_AT[name]:SMALL_AT[name] + SMALL[name]]

        row_g1, row_g2, row_b2 = row[:, 0:D], row[:, D:2 * D], row[:, 2 * D:3 * D]

        x_tok = sb("x_tok", [P, BATCHES, TILES, D])
        xn_tok = sb("xn_tok", [P, BATCHES, TILES, D])
        tx_tok = sb("tx_tok", [P, BATCHES, TILES, D])
        pq = sb("pq", [P, NTILE, 2, D])
        r_tok = sb("r_tok", [P, NTILE, D])
        r_flat = r_tok[:, :, :].rearrange("p n d -> p (n d)")
        first_raw = r_flat[:, 0:640]
        ffn_raw = r_flat[:, 640:640 + 2 * HID]
        ffn_scaled = r_flat[:, 1344:1344 + 2 * HID]
        x1g = sb("x1g", [P, BATCHES, TILES, D])
        x1_hi, x1_lo = sb("x1_hi", [P, BATCHES, SEQ], F32R), sb("x1_lo", [P, BATCHES, SEQ], F32R)

        xT_hi, xT_lo = sb("xT_hi", [P, 2, SEQ], F32R), sb("xT_lo", [P, 2, SEQ], F32R)
        q_stage = sb("q_stage", [P, 2, 2, SEQ])
        eq, qf = q_stage[:, 0], q_stage[:, 1]
        h1 = q_stage
        ek, kf = sb("ek", [P, 3, D]), sb("kf", [P, 3, D])
        v1 = sb("v1", [P, 3, D + 1])
        kv_sb = sb("kv_sb", [P, 2, D + 1])
        u1, x1n = sb("u1", [P, 2, TILES, D]), sb("x1n", [P, 2, TILES, D])
        h2, h3 = sb("h2", [P, 2, SEQ]), sb("h3", [P, 2, SEQ // 2])
        pq_flat = pq[:, :, :, :].rearrange("p n a d -> p (n a d)")

        def in_pq(at, n):
            return pq_flat[:, at * SEQ:(at + n) * SEQ]

        hid = [in_pq(3 * i, 3).rearrange("p (c n) -> p c n", c=CHUNKS) for i in range(2)]
        sg = [in_pq(6 + i, 1) for i in range(2)]
        u2 = [in_pq(8 + i, 1).rearrange("p (t d) -> p t d", t=TILES) for i in range(2)]
        un = [in_pq(10 + i, 1).rearrange("p (t d) -> p t d", t=TILES) for i in range(2)]
        yb = [in_pq(12 + i, 1).rearrange("p (t d) -> p t d", t=TILES) for i in range(2)]

        st = [sb(f"st{i}", [P, BATCHES, TILES, 6]) for i in range(3)]
        mv = [sb(f"mv{i}", [P, BATCHES, TILES, 2]) for i in range(3)]
        nm = [sb(f"nm{i}", [P, BATCHES, TILES]) for i in range(3)]
        ve = [sb(f"ve{i}", [P, BATCHES, TILES]) for i in range(3)]
        rstd = [sb(f"rstd{i}", [P, BATCHES, TILES]) for i in range(3)]
        nmr = [sb(f"nmr{i}", [P, BATCHES, TILES]) for i in range(3)]
        den = sb("den", [P, BATCHES, TILES])
        rden = sb("rden", [P, BATCHES, TILES])
        sum_hi, sum_lo, ctx_sum = sb("sum_hi", [P, BATCHES]), sb("sum_lo", [P, BATCHES]), sb("ctx_sum", [P, BATCHES])
        gh1, gh2, gt = sb("gh1", [P, BATCHES]), sb("gh2", [P, BATCHES]), sb("gt", [P, BATCHES])
        base = sb("base", [P, BATCHES])
        tt = sb("tt", [P, SLOTS, 2, TILES])
        cpl = sb("cpl", [P, SLOTS, 2, TILES])
        ab = sb("ab", [P, PAIRS, 6, 2 * TILES])

        bank = [ctx.enter_context(nc.psum_tensor(f"bank{i}", [P, SEQ], F32)) for i in range(6)]
        bank67 = ctx.enter_context(nc.psum_tensor("bank67", [P, TILES, SEQ // 2], F32))
        ps_xT, ps_x1T, ps_q, ps_k, ps_kv, ps_num = bank[0], bank[0], bank[2], [bank[3], bank[4], bank[1]], bank[5], bank67
        ps_h1, ps_h2 = [bank[3], bank[4]], [bank[1], bank[2]]
        ps_h3 = bank[5][:, 0:SEQ // 2]
        ps_bias = bank[1][:, 0:SEQ // 2].bitcast(BF16)
        ps_gf = bank[2][:, 0:3 * BATCHES].rearrange("p (a b) -> p a b", a=3)
        ps_bf = bank[5][:, 440:440 + 2 * CHUNKS]
        ps_z = bank67[:, 0, 0:SLOTS * 8].rearrange("p (s n) -> p s n", s=SLOTS)
        ps_gate = [bank[0][:], bank67[:, 2:4].rearrange("p a n -> p (a n)")]
        ps_up, ps_down = [bank[3], bank[4]], [bank[1], bank[2]]

        x_loaded = [sem(f"x_loaded{b}") for b in range(BATCHES)]
        first_loaded, small_loaded, ffn_loaded = sem("first_loaded"), sem("small_loaded"), sem("ffn_loaded")
        down_loaded, cols_loaded, rows_loaded = sem("down_loaded"), sem("cols_loaded"), sem("rows_loaded")
        first_ready, bias_ready, ffn_ready, bffn_ps, bffn_ready = [
            sem(n) for n in ("first_ready", "bias_ready", "ffn_ready", "bffn_ps", "bffn_ready")]
        pool_const, cols_ready, consts_ready = sem("pool_const"), sem("cols_ready"), sem("consts_ready")
        eye_ready, split_ready, bias_ps, rstd0_ready = [
            sem(n) for n in ("eye_ready", "split_ready", "bias_ps", "rstd0_ready")]
        dve_step, pool_step, act_step = sem("dve_step"), sem("pool_step"), sem("act_step")
        mean_ready = [sem(f"mean_ready{i}") for i in range(3)]
        rstd_ready = [None, sem("rstd_ready1"), sem("rstd_ready2")]
        xn_ready, tx_ready = sem("xn_ready"), sem("tx_ready")
        xT_ps, xT_hi_ready, xT_lo_ready = sem("xT_ps"), sem("xT_hi_ready"), sem("xT_lo_ready")
        q_ps, eq_ready, qf_ready = sem("q_ps"), sem("eq_ready"), sem("qf_ready")
        k_ps, ek_ready, kf_ready, v_ready, pq_ready = [sem(n) for n in ("k_ps", "ek_ready", "kf_ready", "v_ready", "pq_ready")]
        kv_ps, kv_ready, num_ps, u1_ready = sem("kv_ps"), sem("kv_ready"), sem("num_ps"), sem("u1_ready")
        x1n_ready, x1T_ps, x1_hi_ready, x1_lo_ready, x1g_ready = [
            sem(n) for n in ("x1n_ready", "x1T_ps", "x1_hi_ready", "x1_lo_ready", "x1g_ready")]
        ctx_ready, gf_ps, gf_act, base_ready = sem("ctx_ready"), sem("gf_ps"), sem("gf_act"), sem("base_ready")
        h1_ps, h1_ready, h2_ps, h2_ready = sem("h1_ps"), sem("h1_ready"), sem("h2_ps"), sem("h2_ready")
        h3_ps, h3_ready, z_ps, tt_ready = sem("h3_ps"), sem("h3_ready"), sem("z_ps"), sem("tt_ready")
        r_ready, s_ready, s_dve_ready, ab_ready, ax_ready, o_ready = [
            sem(n) for n in ("r_ready", "s_ready", "s_dve_ready", "ab_ready", "ax_ready", "o_ready")]
        gate_ps, up_ps, sg_ready, hid_ready = sem("gate_ps"), sem("up_ps"), sem("sg_ready"), sem("hid_ready")
        down_ps, u2_ready, un_ready = sem("down_ps"), sem("u2_ready"), sem("un_ready")
        g_ready, mn_ready, y_ready = sem("g_ready"), sem("mn_ready"), sem("y_ready")
        y_stored = [sem("y_stored0"), sem("y_stored1")]

        block = ctx.enter_context(nc.Block())

        @block.sync
        def _(sp):
            sp.dma_start(x_tok[:, 0], x_dram[0]).then_inc(x_loaded[0], 16)
            sp.dma_start(col[:], cols).then_inc(cols_loaded, 16)
            sp.dma_start(small[:], w_small).then_inc(small_loaded, 16)
            sp.dma_start(first_raw[:], w_first).then_inc(first_loaded, 16)
            sp.dma_start(x_tok[:, 1], x_dram[1]).then_inc(x_loaded[1], 16)
            sp.dma_start(x_tok[:, 2], x_dram[2]).then_inc(x_loaded[2], 16)
            sp.dma_start(row[:], rows.to_broadcast([P, row.shape[1]])).then_inc(rows_loaded, 16)
            sp.dma_start(ffn_raw[:], w_ffn).then_inc(ffn_loaded, 16)
            sp.dma_start(wd[:], w_down).then_inc(down_loaded, 16)
            for b in range(3, BATCHES):
                sp.dma_start(x_tok[:, b], x_dram[b]).then_inc(x_loaded[b], 16)
            for b in range(BATCHES):
                sp.wait_ge(y_ready, b + 1)
                sp.dma_start(out_dram[b], yb[b % 2]).then_inc(y_stored[b % 2], 16)
            for i in range(2):
                sp.wait_ge(y_stored[i], 16 * (BATCHES // 2))

        @block.gpsimd
        def _(pool):
            steps = [0]

            def link(ins):
                steps[0] += 1
                ins.then_inc(pool_step, 1)
                pool.wait_ge(pool_step, steps[0])

            def power(i, b):
                pool.wait_ge(mean_ready[i], b + 1)
                link(pool.tensor_scalar(ve[i][:, b], mv[i][:, b, :, 1], 1.0, LN_EPS, ALU.mult, ALU.add))
                return pool.tensor_tensor(rstd[i][:, b], ve[i][:, b], minus_half[:], ALU.pow)

            def norm_x(b):
                link(power(0, b))
                for t in range(TILES):
                    last = pool.tensor_scalar(xn_tok[:, b, t], x_tok[:, b, t], nm[0][:, b, t:t + 1],
                                              rstd[0][:, b, t:t + 1], ALU.add, ALU.mult)
                last.then_inc(xn_ready, 1)

            def rstd_of(i, b):
                link(power(i, b))
                pool.tensor_tensor(nmr[i][:, b], nm[i][:, b], rstd[i][:, b], ALU.mult).then_inc(rstd_ready[i], 1)

            def scale_x1(b):
                pool.wait_ge(x1n_ready, b + 1)
                if b == 0:
                    pool.wait_ge(rows_loaded, 16)
                pool.tensor_tensor(x1g[:, b], x1n[:, b % 2], row_g1.unsqueeze(1).to_broadcast([P, TILES, D]),
                                   ALU.mult).then_inc(x1g_ready, 1)

            def twist_x(b):
                pool.wait_ge(xn_ready, b + 1)
                for to, frm, s in ((0, 2, 1.0), (1, 3, -1.0), (2, 0, -1.0), (3, 1, 1.0)):
                    last = pool.tensor_scalar(tx_tok[:, b, :, to * BLK:(to + 1) * BLK],
                                              xn_tok[:, b, :, frm * BLK:(frm + 1) * BLK], s, 0.0, ALU.mult, ALU.add)
                last.then_inc(tx_ready, 1)

            def s_pair(j):
                pool.wait_ge(r_ready, 2 * (j + 1))
                n0, n1 = 2 * TILES * j, 2 * TILES * j + S_TILES
                c0 = cpl[:, j].rearrange("p a t -> p (a t)")[:, 0:S_TILES].unsqueeze(2).to_broadcast([P, S_TILES, D])
                link(pool.tensor_tensor(pq[:, n0:n1, 0], pq[:, n0:n1, 0], c0, ALU.mult))
                pool.tensor_tensor(pq[:, n0:n1, 1], pq[:, n0:n1, 1], pq[:, n0:n1, 0],
                                   ALU.subtract).then_inc(s_ready, 1)

            def ax_pair(j):
                pool.wait_ge(ab_ready, j + 1)
                pool.wait_ge(tx_ready, 2 * j + 2)
                for b in (2 * j, 2 * j + 1):
                    a = ab[:, j, 2, TILES * (b % 2):TILES * (b % 2) + TILES].unsqueeze(2).to_broadcast([P, TILES, D])
                    pool.tensor_tensor(xn_tok[:, b], xn_tok[:, b], a, ALU.mult).then_inc(ax_ready, 1)

            def gate_rows(b):
                pool.wait_ge(g_ready, b + 1)
                pool.tensor_tensor(tx_tok[:, b], xn_tok[:, b], row_g2.unsqueeze(1).to_broadcast([P, TILES, D]),
                                   ALU.mult)
                link(pool.tensor_tensor(xn_tok[:, b], xn_tok[:, b],
                                        row_b2.unsqueeze(1).to_broadcast([P, TILES, D]), ALU.mult))
                pool.tensor_tensor(x_tok[:, b], x_tok[:, b], xn_tok[:, b], ALU.add).then_inc(mn_ready, 1)

            pool.memset(minus_half[:], -0.5).then_inc(pool_const, 1)
            pool.wait_ge(pool_const, 1)
            power(0, 0).then_inc(rstd0_ready, 1)
            pool.wait_ge(xn_ready, 1)
            norm_x(1)
            for b in range(BATCHES + 2):
                if b + 2 < BATCHES:
                    norm_x(b + 2)
                if b < BATCHES:
                    twist_x(b)
                if b >= 2:
                    rstd_of(1, b - 2)
                if b >= 3:
                    scale_x1(b - 3)
            for j in range(PAIRS):
                s_pair(j)
                if j == 0:
                    scale_x1(BATCHES - 1)
            for j in range(PAIRS):
                ax_pair(j)
            for b in range(BATCHES + 1):
                if b < BATCHES:
                    gate_rows(b)
                if b >= 1:
                    rstd_of(2, b - 1)

        @block.scalar
        def _(act):
            def hi_x(b):
                act.wait_ge(xT_ps, b + 1)
                if b >= 2:
                    act.wait_ge(k_ps, TILES * (b - 1))
                act.activation(xT_hi[:, b % 2], ps_xT[:], ACT.Identity,
                               accum_out=sum_hi[:, b:b + 1]).then_inc(xT_hi_ready, 1)

            def exp_q(b):
                act.wait_ge(q_ps, b + 1)
                if b >= 2:
                    act.wait_ge(qf_ready, b - 1)
                act.activation(eq[:, b % 2], ps_q[:], ACT.Exp, bias=minus_one[:, 0:1]).then_inc(eq_ready, 1)

            def token_tile(n):
                act.wait_ge(k_ps, n + 1)
                if n >= 3:
                    act.wait_ge(kf_ready, n - 2)
                act.activation(ek[:, n % 3], ps_k[n % 3][:, 0:D], ACT.Exp, bias=minus_one[:, 0:1]).then_inc(ek_ready, 1)
                if n >= 3:
                    act.wait_ge(kv_ps, n - 2)
                act.copy(v1[:, n % 3, 0:D], ps_k[n % 3][:, D:2 * D]).then_inc(v_ready, 1)
                act.copy(pq[:, n].rearrange("p a d -> p (a d)"), ps_k[n % 3][:, 2 * D:4 * D]).then_inc(pq_ready, 1)

            def norm_1(b, tiles=range(TILES)):
                act.wait_ge(rstd_ready[1], b + 1)
                if b >= 2:
                    act.wait_ge(x1T_ps, b - 1)
                    act.wait_ge(x1g_ready, b - 1)
                for t in tiles:
                    last = act.activation(x1n[:, b % 2, t], u1[:, b % 2, t], ACT.Identity,
                                          scale=rstd[1][:, b, t:t + 1], bias=nmr[1][:, b, t:t + 1])
                if tiles[-1] == TILES - 1:
                    last.then_inc(x1n_ready, 1)

            def hi_x1(b):
                act.wait_ge(x1T_ps, b + 1)
                act.copy(x1_hi[:, b], ps_x1T[:]).then_inc(x1_hi_ready, 1)

            def global_act(i):
                act.wait_ge(gf_ps, i + 1)
                if i == 2:
                    act.activation(gt[:], ps_gf[:, 2], ACT.Tanh, scale=0.5, bias=half_gb3[:, 0:1]).then_inc(gf_act, 1)
                else:
                    m, dst, name = ((64, gh1, "gc_b1"), (32, gh2, "gc_b2"))[i]
                    act.activation(dst[0:m], ps_gf[0:m, i], ACT.Gelu, scale=1.0 / SEQ if i == 0 else 1.0,
                                   bias=col[0:m, COL[name]:COL[name] + 1]).then_inc(gf_act, 1)

            def gelu_1(s):
                for par in range(2):
                    m = 2 * s + par
                    act.wait_ge(h1_ps, m + 1)
                    if s >= 2:
                        act.wait_ge(h2_ps, s - 1)
                    act.activation(h1[:, s % 2, par], ps_h1[par][:], ACT.Gelu,
                                   bias=col[:, COL["cn_b1"]:COL["cn_b1"] + 1]).then_inc(h1_ready, 1)

            def gelu_2(s):
                act.wait_ge(h2_ps, s + 1)
                if s >= 2:
                    act.wait_ge(h3_ps, s - 1)
                act.activation(h2[:, s % 2], ps_h2[s % 2][:], ACT.Gelu,
                               bias=col[:, COL["cn_b2"]:COL["cn_b2"] + 1]).then_inc(h2_ready, 1)

            def gelu_3(s):
                act.wait_ge(h3_ps, s + 1)
                if s >= 2:
                    act.wait_ge(z_ps, s - 1)
                act.activation(h3[:, s % 2], ps_h3, ACT.Gelu,
                               bias=col[:, COL["cn_b3"]:COL["cn_b3"] + 1]).then_inc(h3_ready, 1)

            def tanh_z(s):
                act.wait_ge(z_ps, s + 1)
                act.activation(tt[:, s].rearrange("p par (ch u) -> p u ch par", ch=2),
                               ps_z[:, s].rearrange("p (u ch par) -> p u ch par", u=2, ch=2), ACT.Tanh,
                               bias=half_b4[:, 0:1], scale=0.5).then_inc(tt_ready, 1)

            def silu_o(b):
                act.wait_ge(o_ready, b + 1)
                act.activation(xn_tok[:, b], xn_tok[:, b], ACT.Silu).then_inc(g_ready, 1)

            def silu_gate(n):
                b, c = divmod(n, CHUNKS)
                act.wait_ge(gate_ps, n + 1)
                if n >= 2:
                    act.wait_ge(hid_ready, n - 1)
                if n == 0:
                    act.wait_ge(bffn_ready, 1)
                m = CHUNK_ROWS[c]
                act.activation(sg[n % 2][0:m], ps_gate[n % 2][0:m], ACT.Silu,
                               bias=bffn[0:m, c:c + 1]).then_inc(sg_ready, 1)

            def norm_2(b):
                act.wait_ge(rstd_ready[2], b + 1)
                if b >= 2:
                    act.wait_ge(y_ready, b - 1)
                for t in range(TILES):
                    last = act.activation(un[b % 2][:, t], u2[b % 2][:, t], ACT.Identity,
                                          scale=rstd[2][:, b, t:t + 1], bias=nmr[2][:, b, t:t + 1])
                last.then_inc(un_ready, 1)

            act.wait_ge(small_loaded, 16)
            act.copy(eye_bf[:], eye).then_inc(eye_ready, 1)
            act.wait_ge(consts_ready, 1)
            hi_x(0)
            for b in range(BATCHES):
                exp_q(b)
                for t in range(TILES):
                    token_tile(TILES * b + t)
                    if t == 0 and b >= 4:
                        hi_x1(b - 4)
                    if t in (1, 3) and b >= 3:
                        norm_1(b - 3, (t - 1, t))
                    if t == 2 and b + 1 < BATCHES:
                        hi_x(b + 1)
            act.wait_ge(cols_ready, 1)
            global_act(0)
            gelu_1(0)
            global_act(1)
            gelu_1(1)
            global_act(2)
            for s in range(SLOTS):
                gelu_2(s)
                if s % 2 == 0 and s < 8:
                    hi_x1(BATCHES - 4 + s // 2)
                if s >= 1:
                    tanh_z(s - 1)
                if s + 2 < SLOTS:
                    gelu_1(s + 2)
                gelu_3(s)
                if s in (0, 2, 4):
                    norm_1(BATCHES - 3 + s // 2)
            tanh_z(SLOTS - 1)
            for b in range(BATCHES + 2):
                if b < BATCHES:
                    silu_gate(CHUNKS * b)
                if b == 0:
                    silu_o(0)
                if b < BATCHES:
                    silu_gate(CHUNKS * b + 1)
                    silu_gate(CHUNKS * b + 2)
                if b >= 2:
                    norm_2(b - 2)
                if b + 1 < BATCHES:
                    silu_o(b + 1)

        @block.vector
        def _(dve):
            steps = [0]

            def mark(ins):
                steps[0] += 1
                ins.then_inc(dve_step, 1)
                return ins

            def link(ins):
                mark(ins)
                dve.wait_ge(dve_step, steps[0])

            def stats(i, b, src):
                for t in range(TILES):
                    last = dve.bn_stats(st[i][:, b, t], src[:, t])
                link(last)
                for t in range(TILES):
                    last = dve.bn_aggr(mv[i][:, b, t], st[i][:, b, t])
                link(last)
                dve.tensor_scalar(nm[i][:, b], mv[i][:, b, :, 0], -1.0, None, ALU.mult).then_inc(mean_ready[i], 1)

            def stats_x(b):
                dve.wait_ge(x_loaded[b], 16)
                stats(0, b, x_tok[:, b])

            def norm_first(b):
                dve.wait_ge(rstd0_ready, 1)
                for t in range(TILES):
                    last = dve.tensor_scalar(xn_tok[:, b, t], x_tok[:, b, t], nm[0][:, b, t:t + 1],
                                             rstd[0][:, b, t:t + 1], ALU.add, ALU.mult)
                last.then_inc(xn_ready, 1)

            def lo_x(b):
                dve.wait_ge(xT_hi_ready, b + 1)
                if b >= 2:
                    dve.wait_ge(k_ps, TILES * (b - 1))
                dve.scalar_tensor_tensor(out=xT_lo[:, b % 2], in0=ps_xT[:], scalar=1.0,
                                         in1=xT_hi[:, b % 2].bitcast(F32), op0=ALU.mult, op1=ALU.subtract,
                                         accum_out=sum_lo[:, b:b + 1]).then_inc(xT_lo_ready, 1)

            def feature_q(b):
                dve.wait_ge(eq_ready, b + 1)
                if b >= 2:
                    dve.wait_ge(num_ps, b - 1)
                dve.scalar_tensor_tensor(out=qf[:, b % 2], in0=eq[:, b % 2], scalar=1.0, in1=ps_q[:],
                                         op0=ALU.min, op1=ALU.max).then_inc(qf_ready, 1)

            def feature_k(n):
                dve.wait_ge(pq_ready, n + 1)
                if n >= 3:
                    dve.wait_ge(kv_ps, n - 2)
                dve.scalar_tensor_tensor(out=kf[:, n % 3], in0=ek[:, n % 3], scalar=1.0, in1=ps_k[n % 3][:, 0:D],
                                         op0=ALU.min, op1=ALU.max).then_inc(kf_ready, 1)

            def copy_kv(b):
                dve.wait_ge(kv_ps, TILES * (b + 1))
                if b >= 2:
                    dve.wait_ge(num_ps, b - 1)
                dve.tensor_copy(kv_sb[:, b % 2], ps_kv[:, 0:D + 1]).then_inc(kv_ready, 1)

            def attend(b, tiles):
                if tiles[0] == 0:
                    invert_den(b)
                for t in tiles:
                    last = dve.scalar_tensor_tensor(out=u1[:, b % 2, t], in0=ps_num[:, t, 0:D],
                                                    scalar=rden[:, b, t:t + 1], in1=xn_tok[:, b, t],
                                                    op0=ALU.mult, op1=ALU.add)
                if tiles[-1] == TILES - 1:
                    last.then_inc(u1_ready, 1)

            def invert_den(b):
                dve.wait_ge(num_ps, b + 1)
                link(dve.tensor_scalar(den[:, b], ps_num[:, :, D], ATTN_EPS, None, ALU.add))
                link(dve.reciprocal(rden[:, b], den[:, b]))
                if b >= 2:
                    dve.wait_ge(x1n_ready, b - 1)

            def stats_u1(b):
                dve.wait_ge(u1_ready, b + 1)
                stats(1, b, u1[:, b % 2])

            def lo_x1(b):
                dve.wait_ge(x1_hi_ready, b + 1)
                dve.tensor_tensor(x1_lo[:, b], ps_x1T[:], x1_hi[:, b].bitcast(F32), ALU.subtract).then_inc(x1_lo_ready, 1)

            def coupling(s):
                j = s % PAIRS
                dve.wait_ge(tt_ready, s + 1)
                if s == 0:
                    dve.wait_ge(base_ready, 1)
                link(dve.scalar_tensor_tensor(out=cpl[:, s], in0=tt[:, s], scalar=gain[:, 1:2],
                                              in1=base[:, 2 * j:2 * j + 2].unsqueeze(2).to_broadcast([P, 2, TILES]),
                                              op0=ALU.mult, op1=ALU.add))

            def next_r(s):
                cycle, j = divmod(s, PAIRS)
                if cycle == 1:
                    dve.wait_ge(s_ready, j + 1)
                    dve.wait_ge(s_dve_ready, j + 1)
                for i in range(2 * TILES):
                    n = 2 * TILES * j + i
                    ins = dve.scalar_tensor_tensor(out=r_tok[:, n], in0=pq[:, n, 1],
                                                    scalar=cpl[:, s, i // TILES, i % TILES:i % TILES + 1],
                                                    in1=pq[:, n, 0] if cycle == 0 else r_tok[:, n],
                                                    op0=ALU.mult, op1=ALU.add)
                    if i % TILES == TILES - 1:
                        ins.then_inc(r_ready, 1)

            def s_rest(j):
                dve.wait_ge(r_ready, 2 * (j + 1))
                c0 = cpl[:, j].rearrange("p a t -> p (a t)")
                link(dve.tensor_scalar(ab[:, j, 4, S_TILES:], c0[:, S_TILES:], -1.0, None, ALU.mult))
                for i in range(S_TILES, 2 * TILES):
                    n = 2 * TILES * j + i
                    last = dve.scalar_tensor_tensor(out=pq[:, n, 1], in0=pq[:, n, 0], scalar=ab[:, j, 4, i:i + 1],
                                                    in1=pq[:, n, 1], op0=ALU.mult, op1=ALU.add)
                last.then_inc(s_dve_ready, 1)

            def scalars_ab(j):
                c0, c1, c2 = [cpl[:, j + PAIRS * n].rearrange("p a t -> p (a t)") for n in range(CYCLES)]
                a1, b1, a, b, t0, t1 = [ab[:, j, i] for i in (0, 1, 2, 3, 4, 5)]
                dve.tensor_tensor(t0, c0, c1, ALU.mult)
                link(dve.tensor_tensor(b1, c0, c1, ALU.add))
                dve.tensor_scalar(a1, t0, -1.0, 1.0, ALU.mult, ALU.add)
                link(dve.tensor_tensor(t1, c2, b1, ALU.mult))
                dve.tensor_tensor(a, a1, t1, ALU.subtract)
                link(dve.tensor_tensor(t0, c2, a1, ALU.mult))
                dve.tensor_tensor(b, b1, t0, ALU.add).then_inc(ab_ready, 1)

            def o3(b):
                j = b // 2
                dve.wait_ge(ax_ready, b + 1)
                for t in range(TILES):
                    i = TILES * (b % 2) + t
                    last = dve.scalar_tensor_tensor(out=xn_tok[:, b, t], in0=tx_tok[:, b, t],
                                                    scalar=ab[:, j, 3, i:i + 1], in1=xn_tok[:, b, t],
                                                    op0=ALU.mult, op1=ALU.add)
                last.then_inc(o_ready, 1)

            def hidden(n):
                b, c = divmod(n, CHUNKS)
                m = CHUNK_ROWS[c]
                dve.wait_ge(up_ps, n + 1)
                dve.wait_ge(sg_ready, n + 1)
                if b >= 2:
                    dve.wait_ge(down_ps, b - 1)
                dve.scalar_tensor_tensor(out=hid[b % 2][0:m, c], in0=ps_up[n % 2][0:m],
                                         scalar=bffn[0:m, CHUNKS + c:CHUNKS + c + 1], in1=sg[n % 2][0:m],
                                         op0=ALU.add, op1=ALU.mult).then_inc(hid_ready, 1)

            def residual_2(b):
                dve.wait_ge(down_ps, b + 1)
                dve.wait_ge(x1g_ready, b + 1)
                if b >= 2:
                    dve.wait_ge(un_ready, b - 1)
                dve.tensor_tensor(u2[b % 2], ps_down[b % 2][:].rearrange("p (t d) -> p t d", t=TILES), x1g[:, b],
                                  ALU.add).then_inc(u2_ready, 1)
                dve.wait_ge(u2_ready, b + 1)
                stats(2, b, u2[b % 2])

            def finish(b):
                dve.wait_ge(un_ready, b + 1)
                dve.wait_ge(mn_ready, b + 1)
                if b >= 2:
                    dve.wait_ge(y_stored[b % 2], 16 * (b // 2))
                link(dve.tensor_tensor(yb[b % 2], un[b % 2], tx_tok[:, b], ALU.mult))
                dve.tensor_tensor(yb[b % 2], yb[b % 2], x_tok[:, b], ALU.add).then_inc(y_ready, 1)

            def split_bias():
                dve.wait_ge(cols_loaded, 16)
                dve.tensor_scalar(bias_col[:, 0:2], col[:, 0:2], 1.0, None, ALU.add)
                dve.tensor_copy(bias_col[:, 2:3], col[:, 2:3])
                link(dve.tensor_tensor(bias_col[:, 3:4], col[:, 3:4], col[:, COL["b1"]:COL["b1"] + 1], ALU.add))
                for part in range(3):
                    last = dve.tensor_copy(bias_split[:, :, part], bias_col[:])
                    if part < 2:
                        link(last)
                        link(dve.tensor_tensor(bias_col[:], bias_col[:], bias_split[:, :, part], ALU.subtract))
                last.then_inc(split_ready, 1)

            dve.memset(minus_one[:], -1.0)
            dve.memset(bias3[:], 0.0)
            dve.memset(ones_bf[:], 1.0)
            dve.memset(v1[:, :, D:D + 1], 1.0)
            for i, s in enumerate((-1.0, 1.0, 1.0, -1.0)):
                last = dve.memset(sign[BLK * i:BLK * (i + 1)], s)
            last.then_inc(consts_ready, 1)
            dve.wait_ge(consts_ready, 1)
            stats_x(0)
            split_bias()
            dve.wait_ge(first_loaded, 16)
            link(dve.tensor_scalar(first_raw[:, 3 * D:4 * D], first_raw[:, 3 * D:4 * D], sign[:, 0:1], None, ALU.mult))
            norm_first(0)
            dve.wait_ge(bias_ps, 1)
            dve.tensor_copy(bias3[0:3], ps_bias[0:3]).then_inc(bias_ready, 1)
            link(dve.tensor_copy(first_hi[:], first_raw[:]))
            dve.tensor_tensor(first_lo[:], first_raw[:], first_hi[:].bitcast(F32), ALU.subtract).then_inc(first_ready, 1)
            lo_x(0)
            stats_x(1)
            dve.tensor_scalar(half_b4[:], col[:, COL["cn_b4"]:COL["cn_b4"] + 1], 0.5, None, ALU.mult)
            dve.tensor_scalar(half_gb3[:], col[:, COL["gc_b3"]:COL["gc_b3"] + 1], 0.5, None, ALU.mult)
            dve.tensor_scalar(gain[:, 0:1], col[:, COL["range"]:COL["range"] + 1], W_GLOBAL, None, ALU.mult)
            dve.tensor_scalar(gain[:, 1:2], col[:, COL["range"]:COL["range"] + 1], W_TOKEN, None,
                              ALU.mult).then_inc(cols_ready, 1)

            stats_x(2)
            for b in range(BATCHES):
                feature_q(b)
                feature_k(TILES * b)
                if b >= 1:
                    copy_kv(b - 1)
                if b >= 4:
                    lo_x1(b - 4)
                feature_k(TILES * b + 1)
                if b >= 2:
                    attend(b - 2, range(TILES))
                feature_k(TILES * b + 2)
                if b + 1 < BATCHES:
                    lo_x(b + 1)
                feature_k(TILES * b + 3)
                if b >= 2:
                    stats_u1(b - 2)
                if b + 3 < BATCHES:
                    stats_x(b + 3)
                if b == 1:
                    dve.wait_ge(ffn_loaded, 16)
                    link(dve.tensor_scalar(ffn_scaled[:], ffn_raw[:], col[:, COL["g1"]:COL["g1"] + 1], None, ALU.mult))
                    link(dve.tensor_copy(ffn_hi[:], ffn_scaled[:]))
                    dve.tensor_tensor(ffn_lo[:], ffn_scaled[:], ffn_hi[:].bitcast(F32),
                                      ALU.subtract).then_inc(ffn_ready, 1)
            dve.wait_ge(xT_lo_ready, BATCHES)
            dve.tensor_tensor(ctx_sum[:], sum_hi[:], sum_lo[:], ALU.add).then_inc(ctx_ready, 1)
            copy_kv(BATCHES - 1)
            attend(BATCHES - 2, range(TILES))
            dve.wait_ge(bffn_ps, 1)
            for c, m in enumerate(CHUNK_ROWS):
                last = dve.tensor_tensor(bffn[0:m, c::CHUNKS], ps_bf[0:m, c::CHUNKS],
                                         col[0:m, COL["bg0"] + c::CHUNKS], ALU.add)
            last.then_inc(bffn_ready, 1)
            stats_u1(BATCHES - 2)
            attend(BATCHES - 1, range(TILES))
            stats_u1(BATCHES - 1)
            lo_x1(BATCHES - 4)
            dve.wait_ge(gf_act, 3)
            dve.tensor_scalar(base[:], gt[:], gain[:, 0:1], BASE_COUPLING, ALU.mult, ALU.add).then_inc(base_ready, 1)
            for s in range(SLOTS):
                coupling(s)
                if s < 2 * PAIRS:
                    next_r(s)
                    if s < PAIRS:
                        s_rest(s)
                    if s in (1, 3, 5):
                        lo_x1(BATCHES - 3 + s // 2)
                else:
                    scalars_ab(s - 2 * PAIRS)
            for b in range(2):
                o3(b)
            for b in range(BATCHES + 3):
                if b < BATCHES:
                    hidden(CHUNKS * b)
                if b >= 3:
                    finish(b - 3)
                if b < BATCHES:
                    hidden(CHUNKS * b + 1)
                if b + 2 < BATCHES:
                    o3(b + 2)
                if b < BATCHES:
                    hidden(CHUNKS * b + 2)
                if 1 <= b <= BATCHES:
                    residual_2(b - 1)

        @block.tensor
        def _(pe):
            def transposes(dst, src):
                for t in range(TILES):
                    last = pe.transpose(dst[:, t * P:(t + 1) * P], src[:, t], eye)
                return last

            def transpose_x(b):
                pe.wait_ge(xn_ready, b + 1)
                if b >= 1:
                    pe.wait_ge(xT_lo_ready, b)
                if b >= 5:
                    pe.wait_ge(x1_lo_ready, b - 4)
                transposes(ps_xT, xn_tok[:, b]).then_inc(xT_ps, 1)

            def project_q(b):
                pe.wait_ge(xT_lo_ready, b + 1)
                if b == 0:
                    pe.wait_ge(first_ready, 1)
                    pe.wait_ge(bias_ready, 1)
                if b >= 1:
                    pe.wait_ge(qf_ready, b)
                hi, lo = xT_hi[:, b % 2], xT_lo[:, b % 2]
                wq = slice(4 * D, 5 * D)
                pe.matmul(ps_q[:], first_hi[:, wq], hi, start=True, stop=False)
                pe.matmul(ps_q[:], first_hi[:, wq], lo, start=False, stop=False)
                pe.matmul(ps_q[:], first_lo[:, wq], hi, start=False, stop=False)
                pe.matmul(ps_q[:], bias3[:, 0:D], ones_bf[:], start=False, stop=True).then_inc(q_ps, 1)

            def project_tokens(n):
                b, t = divmod(n, TILES)
                if n >= 3:
                    pe.wait_ge(kf_ready, n - 2)
                dst = ps_k[n % 3]
                hi, lo = xT_hi[:, b % 2, t * P:(t + 1) * P], xT_lo[:, b % 2, t * P:(t + 1) * P]
                pe.matmul(dst[:], hi, first_hi[:, 0:4 * D], start=True, stop=False)
                pe.matmul(dst[:], hi, first_lo[:, 0:4 * D], start=False, stop=False)
                pe.matmul(dst[:, 0:2 * D], ones_bf[:, 0:P], bias3[:, D:3 * D], start=False, stop=False)
                pe.matmul(dst[:], lo, first_hi[:, 0:4 * D], start=False, stop=True).then_inc(k_ps, 1)

            def sum_kv(n):
                b, t = divmod(n, TILES)
                pe.wait_ge(kf_ready, n + 1)
                pe.wait_ge(v_ready, n + 1)
                if t == 0 and b >= 1:
                    pe.wait_ge(kv_ready, b)
                pe.matmul(ps_kv[:, 0:D + 1], kf[:, n % 3], v1[:, n % 3], start=(t == 0),
                          stop=(t == TILES - 1)).then_inc(kv_ps, 1)

            def numerator(b):
                pe.wait_ge(kv_ready, b + 1)
                pe.wait_ge(qf_ready, b + 1)
                if b >= 1:
                    pe.wait_ge(u1_ready, b)
                for t in range(TILES):
                    last = pe.matmul(ps_num[:, t, 0:D + 1], qf[:, b % 2, t * P:(t + 1) * P], kv_sb[:, b % 2],
                                     start=True, stop=True)
                last.then_inc(num_ps, 1)

            def transpose_x1(b):
                pe.wait_ge(x1n_ready, b + 1)
                if b >= 1:
                    pe.wait_ge(x1_lo_ready, b)
                pe.wait_ge(xT_lo_ready, min(b + 5, BATCHES))
                transposes(ps_x1T, x1n[:, b % 2]).then_inc(x1T_ps, 1)

            def layer_1(s):
                cycle, j = divmod(s, PAIRS)
                for par in range(2):
                    m = 2 * s + par
                    if cycle >= 1:
                        pe.wait_ge(r_ready, m - 2 * PAIRS + 1)
                    if m >= 2:
                        pe.wait_ge(h1_ready, m - 1)
                    n0 = 2 * TILES * j + TILES * par
                    src = pq[:, n0:n0 + TILES, 0] if cycle == 0 else r_tok[:, n0:n0 + TILES]
                    transposes(ps_h1[par], src).then_inc(h1_ps, 1)

            def layer_2(s):
                pe.wait_ge(h1_ready, 2 * s + 2)
                if s >= 2:
                    pe.wait_ge(h2_ready, s - 1)
                for par in range(2):
                    last = pe.matmul(ps_h2[s % 2][64 * par:64 * par + 64, :], sm("cn_w2"), h1[:, s % 2, par],
                                     start=True, stop=True)
                last.then_inc(h2_ps, 1)

            def layer_3(s):
                pe.wait_ge(h2_ready, s + 1)
                if s == 0:
                    pe.wait_ge(bffn_ready, 1)
                else:
                    pe.wait_ge(h3_ready, s)
                for ch in range(2):
                    last = pe.matmul(ps_h3[64 * ch:64 * ch + 64, :], sm("cn_w3"),
                                     h2[:, s % 2, ch * 256:(ch + 1) * 256], start=True, stop=True)
                last.then_inc(h3_ps, 1)

            def layer_4(s):
                pe.wait_ge(h3_ready, s + 1)
                if s == 0:
                    pe.wait_ge(u1_ready, BATCHES)
                else:
                    pe.wait_ge(tt_ready, s)
                for u in range(2):
                    last = pe.matmul(ps_z[:, s, 4 * u:4 * u + 4], h3[:, s % 2, u * P:(u + 1) * P], sm("cn_w4"),
                                     start=True, stop=True)
                last.then_inc(z_ps, 1)

            def global_layer(i):
                if i == 0:
                    pe.wait_ge(ctx_ready, 1)
                    pe.matmul(ps_gf[0:64, 0], sm("gc_w1"), ctx_sum[:], start=True, stop=True).then_inc(gf_ps, 1)
                else:
                    pe.wait_ge(gf_act, i)
                    k, m, src, w = ((64, 32, gh1, "gc_w2"), (32, P, gh2, "gc_w3"))[i - 1]
                    pe.matmul(ps_gf[0:m, i], sm(w, k), src[0:k], start=True, stop=True).then_inc(gf_ps, 1)

            def ffn_bias():
                pe.wait_ge(ffn_loaded, 16)
                pe.wait_ge(cols_loaded, 16)
                for i in range(2 * CHUNKS):
                    k, c = divmod(i, CHUNKS)
                    m = CHUNK_ROWS[c]
                    last = pe.matmul(ps_bf[0:m, i:i + 1], ffn_raw[:, k * HID + c * P:k * HID + c * P + m],
                                     col[:, COL["b1"]:COL["b1"] + 1], start=True, stop=True)
                last.then_inc(bffn_ps, 1)

            def gate_up(n):
                b, c = divmod(n, CHUNKS)
                m = CHUNK_ROWS[c]
                if n >= 2:
                    pe.wait_ge(sg_ready, n - 1)
                for k, (dst, done) in enumerate(((ps_gate, gate_ps), (ps_up, up_ps))):
                    if k == 1 and n >= 2:
                        pe.wait_ge(hid_ready, n - 1)
                    w = slice(k * HID + c * P, k * HID + c * P + m)
                    pe.matmul(dst[n % 2][0:m], ffn_hi[:, w], x1_hi[:, b], start=True, stop=False)
                    pe.matmul(dst[n % 2][0:m], ffn_hi[:, w], x1_lo[:, b], start=False, stop=False)
                    pe.matmul(dst[n % 2][0:m], ffn_lo[:, w], x1_hi[:, b], start=False, stop=True).then_inc(done, 1)

            def down(b, tiles):
                pe.wait_ge(hid_ready, CHUNKS * (b + 1))
                if b >= 2:
                    pe.wait_ge(u2_ready, b - 1)
                dst = ps_down[b % 2]
                for t in tiles:
                    pe.matmul(dst[:, t * P:(t + 1) * P], ones_bf[:, 0:P], bias3[:, 3 * D:4 * D], start=True, stop=False)
                    for c, m in enumerate(CHUNK_ROWS):
                        last = pe.matmul(dst[:, t * P:(t + 1) * P], hid[b % 2][0:m, c, t * P:(t + 1) * P],
                                         wd[0:m, c], start=False, stop=(c == CHUNKS - 1))
                if tiles[-1] == TILES - 1:
                    last.then_inc(down_ps, 1)

            pe.wait_ge(small_loaded, 16)
            pe.wait_ge(eye_ready, 1)
            pe.wait_ge(split_ready, 1)
            for i in range(4):
                last = pe.transpose(ps_bias[0:3, i * D:(i + 1) * D], bias_split[:, i, 0:3], eye_bf[:])
            last.then_inc(bias_ps, 1)
            transpose_x(0)
            for b in range(BATCHES):
                project_q(b)
                for t in range(TILES):
                    n = TILES * b + t
                    project_tokens(n)
                    if t == 0 and b >= 4:
                        transpose_x1(b - 4)
                    if n >= 2:
                        sum_kv(n - 2)
                    if t == 2 and b + 1 < BATCHES:
                        transpose_x(b + 1)
                    if t == 3 and b >= 1:
                        numerator(b - 1)
            sum_kv(NTILE - 2)
            sum_kv(NTILE - 1)
            pe.wait_ge(qf_ready, BATCHES)
            global_layer(0)
            pe.wait_ge(kf_ready, NTILE)
            layer_1(0)
            numerator(BATCHES - 1)
            global_layer(1)
            layer_1(1)
            ffn_bias()
            global_layer(2)
            for s in range(SLOTS):
                if s == 1:
                    pe.wait_ge(gf_act, 3)
                layer_2(s)
                if s % 2 == 0 and s < 8:
                    transpose_x1(BATCHES - 4 + s // 2)
                if s >= 1:
                    layer_4(s - 1)
                if s + 2 < SLOTS:
                    layer_1(s + 2)
                if s == SLOTS - 1:
                    pe.wait_ge(h1_ready, 2 * SLOTS)
                    pe.wait_ge(ffn_ready, 1)
                    pe.wait_ge(x1_lo_ready, BATCHES)
                    gate_up(0)
                layer_3(s)
            gate_up(1)
            layer_4(SLOTS - 1)
            pe.wait_ge(h2_ready, SLOTS)
            pe.wait_ge(down_loaded, 16)
            for b in range(BATCHES + 1):
                for c in range(CHUNKS):
                    if b < BATCHES and CHUNKS * b + c >= 2:
                        gate_up(CHUNKS * b + c)
                    if b >= 1 and c < 2:
                        down(b - 1, (2 * c, 2 * c + 1))


def kernel(**inputs):
    import numpy as np
    import concourse.bacc as bacc
    from concourse.bass_utils import run_bass_kernel_spmd

    a = {k: np.asarray(v) for k, v in inputs.items()}
    w = {k.split("_", 2)[2]: v for k, v in a.items() if k.startswith("L0_ffn")}
    t = {k.split("_", 2)[2]: v for k, v in a.items() if k.startswith("L0_attn")}
    f32 = np.float32

    def padded(v, rows, at=0):
        out = np.zeros((rows,) + v.shape[1:], f32)
        out[at:at + v.shape[0]] = v
        return out

    wqkv = t["Wqkv"]
    w_first = np.concatenate([wqkv[:, D:3 * D], w["cn_w1"],
                              np.concatenate([w["cn_w1"][2 * BLK:], w["cn_w1"][:2 * BLK]]), wqkv[:, 0:D]], axis=1)
    w3 = np.zeros((P, 64), f32)
    w4 = np.zeros((P, 4), f32)
    for i in range(2):
        w3[64 * i:64 * i + 64, 32 * i:32 * i + 32] = w["cn_w3"]
    for i in range(4):
        w4[32 * i:32 * i + 32, i:i + 1] = w["cn_w4"]
    w_small = np.concatenate([w["cn_w2"], w3, w4, w["gc_w1"], padded(w["gc_w2"], P),
                              padded(np.repeat(w["gc_w3"], P, axis=1), P), np.eye(P, dtype=f32)], axis=1)
    w_ffn = np.concatenate([t["Wg"], t["Wu"]], axis=1)
    w_down = padded(t["Wd"], CHUNKS * P).reshape(CHUNKS, P, D).transpose(1, 0, 2)
    cols = [w["cn_b1"], np.tile(w["cn_b2"], 2), np.tile(w["cn_b3"], 4), np.repeat(w["cn_b4"], P),
            np.repeat(w["adaptive_range"], P), padded(w["gc_b1"], P), padded(w["gc_b2"], P),
            np.repeat(w["gc_b3"], P), t["g1"], t["b1"]]
    cols = list(t["bqkv"].reshape(3, D)) + [t["bd"]] + cols
    for name in ("bg", "bu"):
        cols += list(padded(t[name], CHUNKS * P).reshape(CHUNKS, P))
    rows = np.concatenate([t["g1"], t["g2"], t["b2"]])[None]
    sent = {"x": t["x"], "w_first": w_first, "w_small": w_small, "w_ffn": w_ffn, "w_down": w_down,
            "cols": np.stack(cols, axis=1), "rows": rows}

    nc = bacc.Bacc("TRN2", target_bir_lowering=False, num_devices=1)
    arrays, args = {}, []
    for name, v in sent.items():
        v = np.ascontiguousarray(v)
        arrays[f"in_{name}"] = v
        args.append(nc.dram_tensor(f"in_{name}", v.shape, mybir.dt.from_np(v.dtype), kind="ExternalInput").ap())
    out = nc.dram_tensor("out", sent["x"].shape, F32, kind="ExternalOutput").ap()
    gated_block(nc, *args, out)
    result = run_bass_kernel_spmd(nc, [arrays], core_ids=[0])
    return result.results[0]["out"]
```

```python
from contextlib import ExitStack

import concourse.bass as bass
from concourse import mybir

F32 = mybir.dt.float32
F32R = mybir.dt.float32r
BF16 = mybir.dt.bfloat16
ALU = mybir.AluOpType
ACT = mybir.ActivationFunctionType

P = 128
BATCHES, SEQ, D = 8, 512, 128
TILES = SEQ // P
NTILE = BATCHES * TILES
HID = 2 * 512 // 3
CHUNKS = -(-HID // P)
CHUNK_ROWS = [min(P, HID - c * P) for c in range(CHUNKS)]
ACT_NORMS = 5
PAIRS = BATCHES // 2
CYCLES = 3
HALVES = ((0, 1), (2, 3))
SLOTS = CYCLES * PAIRS
LN_EPS, ATTN_EPS = 1e-5, 1e-6
BASE_COUPLING, W_GLOBAL, W_TOKEN = 0.1, 0.7, 0.3
BLK = D // 4

COLS = ["bq", "bk", "bv", "bd", "cn_b1", "cn_b2", "cn_b3", "cn_b4", "range", "gc_b1", "gc_b2", "gc_b3", "g1", "b1"] + \
    [f"bg{c}" for c in range(CHUNKS)] + [f"bu{c}" for c in range(CHUNKS)]
COL = {name: i for i, name in enumerate(COLS)}
SMALL = {"cn_w2": 64, "cn_w3": 64, "cn_w4": 4, "gc_w1": 64, "gc_w2": 32, "gc_w3": P, "eye": P}
SMALL_AT = {n: sum(list(SMALL.values())[:i]) for i, n in enumerate(SMALL)}


def gated_block(nc, x, w_first, w_small, w_ffn, w_down, cols, rows, out):
    x_dram = x.rearrange("b (p t) d -> b p (t d)", t=TILES)
    out_dram = out.rearrange("b (p t) d -> b p (t d)", t=TILES)

    with ExitStack() as ctx:
        def sb(name, shape, dt=F32):
            return ctx.enter_context(nc.sbuf_tensor(name, shape, dt))

        def sem(name):
            return ctx.enter_context(nc.semaphore(name))

        first_hi, first_lo = sb("first_hi", [P, 640], F32R), sb("first_lo", [P, 640], F32R)
        small = sb("small", [P, sum(SMALL.values())])
        ffn_hi, ffn_lo = sb("ffn_hi", [P, 2 * HID], F32R), sb("ffn_lo", [P, 2 * HID], F32R)
        wd = sb("wd", [P, CHUNKS, D])
        col = sb("col", [P, len(COLS)])
        row = sb("row", [P, 3 * D])
        bias3 = sb("bias3", [P, 384 + D], BF16)
        bias_col = sb("bias_col", [P, 4])
        bias_split = sb("bias_split", [P, 4, 4], BF16)
        eye_bf = sb("eye_bf", [P, P], BF16)
        ones_bf = sb("ones_bf", [P, SEQ], BF16)
        sign = sb("sign", [P, 1])
        minus_one = sb("minus_one", [P, 1])
        minus_half = sb("minus_half", [P, TILES])
        half_b4 = sb("half_b4", [P, 1])
        half_gb3 = sb("half_gb3", [P, 1])
        gain = sb("gain", [P, 2])
        bffn = sb("bffn", [P, 2 * CHUNKS])

        eye = small[:, SMALL_AT["eye"]:SMALL_AT["eye"] + P]

        def sm(name, rows_=P):
            return small[0:rows_, SMALL_AT[name]:SMALL_AT[name] + SMALL[name]]

        row_g1, row_g2, row_b2 = row[:, 0:D], row[:, D:2 * D], row[:, 2 * D:3 * D]

        x_tok = sb("x_tok", [P, BATCHES, TILES, D])
        xn_tok = sb("xn_tok", [P, BATCHES, TILES, D])
        tx_tok = sb("tx_tok", [P, BATCHES, TILES, D])
        pq = sb("pq", [P, NTILE, 2, D])
        r_tok = sb("r_tok", [P, NTILE, D])
        r_flat = r_tok[:, :, :].rearrange("p n d -> p (n d)")
        first_raw = r_flat[:, 0:640]
        ffn_raw = r_flat[:, 640:640 + 2 * HID]
        ffn_scaled = r_flat[:, 1344:1344 + 2 * HID]
        x1g = sb("x1g", [P, BATCHES, TILES, D])
        x1_hi, x1_lo = sb("x1_hi", [P, BATCHES, SEQ], F32R), sb("x1_lo", [P, BATCHES, SEQ], F32R)

        xT_hi, xT_lo = sb("xT_hi", [P, 2, SEQ], F32R), sb("xT_lo", [P, 2, SEQ], F32R)
        q_stage = sb("q_stage", [P, 2, 2, SEQ])
        eq, qf = q_stage[:, 0], q_stage[:, 1]
        h1 = q_stage
        ek, kf = sb("ek", [P, 3, D]), sb("kf", [P, 3, D])
        v1 = sb("v1", [P, 3, D + 1])
        kv_sb = sb("kv_sb", [P, 2, D + 1])
        u1, x1n = sb("u1", [P, 2, TILES, D]), sb("x1n", [P, 2, TILES, D])
        h2, h3 = sb("h2", [P, 2, SEQ]), sb("h3", [P, 2, SEQ // 2])
        pq_flat = pq[:, :, :, :].rearrange("p n a d -> p (n a d)")

        def in_pq(at, n):
            return pq_flat[:, at * SEQ:(at + n) * SEQ]

        hid = [in_pq(3 * i, 3).rearrange("p (c n) -> p c n", c=CHUNKS) for i in range(2)]
        sg = [in_pq(6 + i, 1) for i in range(2)]
        u2 = [in_pq(8 + i, 1).rearrange("p (t d) -> p t d", t=TILES) for i in range(2)]
        un = [in_pq(10 + i, 1).rearrange("p (t d) -> p t d", t=TILES) for i in range(2)]
        yb = [in_pq(12 + i, 1).rearrange("p (t d) -> p t d", t=TILES) for i in range(2)]

        st = [sb(f"st{i}", [P, BATCHES, TILES, 6]) for i in range(3)]
        mv = [sb(f"mv{i}", [P, BATCHES, TILES, 2]) for i in range(3)]
        nm = [sb(f"nm{i}", [P, BATCHES, TILES]) for i in range(3)]
        ve = [sb(f"ve{i}", [P, BATCHES, TILES]) for i in range(3)]
        rstd = [sb(f"rstd{i}", [P, BATCHES, TILES]) for i in range(3)]
        nmr = [sb(f"nmr{i}", [P, BATCHES, TILES]) for i in range(3)]
        den = sb("den", [P, BATCHES, TILES])
        rden = sb("rden", [P, BATCHES, TILES])
        sum_hi, sum_lo, ctx_sum = sb("sum_hi", [P, BATCHES]), sb("sum_lo", [P, BATCHES]), sb("ctx_sum", [P, BATCHES])
        gh1, gh2, gt = sb("gh1", [P, BATCHES]), sb("gh2", [P, BATCHES]), sb("gt", [P, BATCHES])
        base = sb("base", [P, BATCHES])
        tt = sb("tt", [P, SLOTS, 2, TILES])
        cpl = sb("cpl", [P, SLOTS, 2, TILES])
        ab = sb("ab", [P, PAIRS, 6, 2 * TILES])

        bank = [ctx.enter_context(nc.psum_tensor(f"bank{i}", [P, SEQ], F32)) for i in range(6)]
        bank67 = ctx.enter_context(nc.psum_tensor("bank67", [P, TILES, SEQ // 2], F32))
        ps_xT, ps_x1T, ps_q, ps_k, ps_kv, ps_num = bank[0], bank[0], bank[2], [bank[3], bank[4], bank[1]], bank[5], bank67
        ps_h1, ps_h2 = [bank[3], bank[4]], [bank[1], bank[2]]
        ps_h3 = bank[5][:, 0:SEQ // 2]
        ps_bias = bank[1][:, 0:SEQ // 2].bitcast(BF16)
        ps_gf = bank[2][:, 0:3 * BATCHES].rearrange("p (a b) -> p a b", a=3)
        ps_bf = bank[5][:, 440:440 + 2 * CHUNKS]
        ps_z = bank67[:, 0, 0:SLOTS * 8].rearrange("p (s n) -> p s n", s=SLOTS)
        ps_gate = [bank[0][:], bank67[:, 2:4].rearrange("p a n -> p (a n)")]
        ps_up, ps_down = [bank[3], bank[4]], [bank[1], bank[2]]
        ps_last = [bank[2], bank[5], bank[0], bank[3]]

        x_loaded = [sem(f"x_loaded{b}") for b in range(BATCHES)]
        first_loaded, small_loaded, ffn_loaded = sem("first_loaded"), sem("small_loaded"), sem("ffn_loaded")
        down_loaded, cols_loaded, rows_loaded = sem("down_loaded"), sem("cols_loaded"), sem("rows_loaded")
        sign_ready, first_hi_ready, centred = sem("sign_ready"), sem("first_hi_ready"), sem("centred")
        first_ready, bias_ready, ffn_ready, bffn_ps, bffn_ready = [
            sem(n) for n in ("first_ready", "bias_ready", "ffn_ready", "bffn_ps", "bffn_ready")]
        ffn_step, pool_const, cols_ready, consts_ready = sem("ffn_step"), sem("pool_const"), sem("cols_ready"), sem("consts_ready")
        eye_ready, split_ready, bias_ps, rstd0_ready = [
            sem(n) for n in ("eye_ready", "split_ready", "bias_ps", "rstd0_ready")]
        dve_step, pool_step = sem("dve_step"), sem("pool_step")
        st_ready, mv_ready, mean_ready = [[sem(f"{n}{i}") for i in range(3)] for n in ("st_ready", "mv_ready", "mean_ready")]
        rstd_ready = [None, sem("rstd_ready1"), sem("rstd_ready2")]
        xn_ready, tx_ready = sem("xn_ready"), sem("tx_ready")
        xT_ps, xT_hi_ready, xT_lo_ready = sem("xT_ps"), sem("xT_hi_ready"), sem("xT_lo_ready")
        q_ps, eq_ready, qf_ready = sem("q_ps"), sem("eq_ready"), sem("qf_ready")
        k_ps, ek_ready, kf_ready, v_ready, pq_ready = [sem(n) for n in ("k_ps", "ek_ready", "kf_ready", "v_ready", "pq_ready")]
        kv_ps, kv_ready, num_ps, u1_ready = sem("kv_ps"), sem("kv_ready"), sem("num_ps"), sem("u1_ready")
        den_ready, rden_ready, x1n_ready, x1T_ps, x1_hi_ready, x1_lo_ready, x1g_ready = [
            sem(n) for n in ("den_ready", "rden_ready", "x1n_ready", "x1T_ps", "x1_hi_ready", "x1_lo_ready", "x1g_ready")]
        ctx_ready, gf_ps, gf_act, base_ready = sem("ctx_ready"), sem("gf_ps"), sem("gf_act"), sem("base_ready")
        h1_ps, h1_ready, h2_ps, h2_ready = sem("h1_ps"), sem("h1_ready"), sem("h2_ps"), sem("h2_ready")
        h3_ps, h3_ready, z_ps, tt_ready = sem("h3_ps"), sem("h3_ready"), sem("z_ps"), sem("tt_ready")
        r_ready, s_ready, cpl_ready, ax_ready, o_ready = [
            sem(n) for n in ("r_ready", "s_ready", "cpl_ready", "ax_ready", "o_ready")]
        gate_ps, up_ps, sg_ready, hid_ready = sem("gate_ps"), sem("up_ps"), sem("sg_ready"), sem("hid_ready")
        down_ps, u2_ready, un_ready = sem("down_ps"), sem("u2_ready"), sem("un_ready")
        g_ready, mn_ready, y_ready = sem("g_ready"), sem("mn_ready"), sem("y_ready")
        y_stored = [sem("y_stored0"), sem("y_stored1")]

        block = ctx.enter_context(nc.Block())

        @block.sync
        def _(sp):
            sp.dma_start(x_tok[:, 0], x_dram[0]).then_inc(x_loaded[0], 16)
            sp.dma_start(col[:], cols).then_inc(cols_loaded, 16)
            sp.dma_start(small[:], w_small).then_inc(small_loaded, 16)
            sp.dma_start(first_raw[:], w_first).then_inc(first_loaded, 16)
            sp.dma_start(x_tok[:, 1], x_dram[1]).then_inc(x_loaded[1], 16)
            sp.dma_start(x_tok[:, 2], x_dram[2]).then_inc(x_loaded[2], 16)
            sp.dma_start(row[:], rows.to_broadcast([P, row.shape[1]])).then_inc(rows_loaded, 16)
            sp.dma_start(ffn_raw[:], w_ffn).then_inc(ffn_loaded, 16)
            sp.dma_start(wd[:], w_down).then_inc(down_loaded, 16)
            for b in range(3, BATCHES):
                sp.dma_start(x_tok[:, b], x_dram[b]).then_inc(x_loaded[b], 16)
            for b in range(BATCHES - 1):
                sp.wait_ge(y_ready, b + 1)
                sp.dma_start(out_dram[b], yb[b % 2]).then_inc(y_stored[b % 2], 16)
            b = BATCHES - 1
            for half, tiles in enumerate(HALVES):
                sp.wait_ge(y_ready, b + half + 1)
                sp.dma_start(out_dram[b][:, tiles[0] * D:(tiles[-1] + 1) * D],
                             u2[b % 2][:, tiles[0]:tiles[-1] + 1].rearrange("p t d -> p (t d)")).then_inc(y_stored[b % 2], 16)
            sp.wait_ge(y_stored[0], 16 * (BATCHES // 2))
            sp.wait_ge(y_stored[1], 16 * (BATCHES // 2 + 1))

        @block.gpsimd
        def _(pool):
            steps = [0]

            def link(ins):
                steps[0] += 1
                ins.then_inc(pool_step, 1)
                pool.wait_ge(pool_step, steps[0])

            def power(i, b, tiles=range(TILES), half=0):
                pool.wait_ge(mean_ready[i], b + half + 1)
                ts = slice(tiles[0], tiles[-1] + 1)
                link(pool.tensor_scalar(ve[i][:, b, ts], mv[i][:, b, ts, 1], 1.0, LN_EPS, ALU.mult, ALU.add))
                return pool.tensor_tensor(rstd[i][:, b, ts], ve[i][:, b, ts], minus_half[:, ts], ALU.pow)

            def norm_x(b):
                link(power(0, b))
                for t in range(TILES):
                    last = pool.tensor_scalar(xn_tok[:, b, t], x_tok[:, b, t], nm[0][:, b, t:t + 1],
                                              rstd[0][:, b, t:t + 1], ALU.add, ALU.mult)
                last.then_inc(xn_ready, 1)

            def rstd_of(i, b):
                link(power(i, b))
                pool.tensor_tensor(nmr[i][:, b], nm[i][:, b], rstd[i][:, b], ALU.mult).then_inc(rstd_ready[i], 1)

            def finish(b):
                pool.wait_ge(un_ready, b + 1)
                pool.wait_ge(y_ready, b)
                pool.wait_ge(y_stored[b % 2], 16 * (b // 2))
                link(pool.tensor_tensor(yb[b % 2], un[b % 2], tx_tok[:, b], ALU.mult))
                pool.tensor_tensor(yb[b % 2], yb[b % 2], x_tok[:, b], ALU.add).then_inc(y_ready, 1)

            def norm_x1(b):
                pool.wait_ge(rstd_ready[1], b + 1)
                pool.wait_ge(x1n_ready, b)
                pool.wait_ge(x1T_ps, b - 1)
                pool.wait_ge(x1g_ready, b - 1)
                for t in range(TILES):
                    last = pool.tensor_scalar(x1n[:, b % 2, t], u1[:, b % 2, t], nm[1][:, b, t:t + 1],
                                              rstd[1][:, b, t:t + 1], ALU.add, ALU.mult)
                last.then_inc(x1n_ready, 1)

            def scale_x1(b):
                pool.wait_ge(x1n_ready, b + 1)
                if b == 0:
                    pool.wait_ge(rows_loaded, 16)
                pool.tensor_tensor(x1g[:, b], x1n[:, b % 2], row_g1.unsqueeze(1).to_broadcast([P, TILES, D]),
                                   ALU.mult).then_inc(x1g_ready, 1)

            def twist_x(b):
                pool.wait_ge(xn_ready, b + 1)
                for to, frm, s in ((0, 2, 1.0), (1, 3, -1.0), (2, 0, -1.0), (3, 1, 1.0)):
                    last = pool.tensor_scalar(tx_tok[:, b, :, to * BLK:(to + 1) * BLK],
                                              xn_tok[:, b, :, frm * BLK:(frm + 1) * BLK], s, 0.0, ALU.mult, ALU.add)
                last.then_inc(tx_ready, 1)

            def s_pair(j):
                pool.wait_ge(r_ready, 2 * (j + 1))
                n0, n1 = 2 * TILES * j, 2 * TILES * (j + 1)
                c0 = cpl[:, j].rearrange("p a t -> p (a t)").unsqueeze(2).to_broadcast([P, 2 * TILES, D])
                link(pool.tensor_tensor(pq[:, n0:n1, 0], pq[:, n0:n1, 0], c0, ALU.mult))
                pool.tensor_tensor(pq[:, n0:n1, 1], pq[:, n0:n1, 1], pq[:, n0:n1, 0],
                                   ALU.subtract).then_inc(s_ready, 1)

            def scalars_2(j):
                pool.wait_ge(cpl_ready, PAIRS + j + 1)
                c0, c1 = [cpl[:, j + PAIRS * n].rearrange("p a t -> p (a t)") for n in range(2)]
                a1, b1, t0 = [ab[:, j, i] for i in (0, 1, 4)]
                link(pool.tensor_tensor(t0, c0, c1, ALU.mult))
                pool.tensor_scalar(a1, t0, -1.0, 1.0, ALU.mult, ALU.add)
                link(pool.tensor_tensor(b1, c0, c1, ALU.add))

            def scalars_3(j):
                pool.wait_ge(cpl_ready, 2 * PAIRS + j + 1)
                c2 = cpl[:, j + 2 * PAIRS].rearrange("p a t -> p (a t)")
                a1, b1, a, b, t0, t1 = [ab[:, j, i] for i in range(6)]
                pool.tensor_tensor(t1, c2, b1, ALU.mult)
                link(pool.tensor_tensor(t0, c2, a1, ALU.mult))
                pool.tensor_tensor(a, a1, t1, ALU.subtract)
                link(pool.tensor_tensor(b, b1, t0, ALU.add))

            def ax_pair(j):
                pool.wait_ge(tx_ready, 2 * j + 2)
                for b in (2 * j, 2 * j + 1):
                    a = ab[:, j, 2, TILES * (b % 2):TILES * (b % 2) + TILES].unsqueeze(2).to_broadcast([P, TILES, D])
                    pool.tensor_tensor(xn_tok[:, b], xn_tok[:, b], a, ALU.mult).then_inc(ax_ready, 1)

            def gate_rows(b):
                pool.wait_ge(g_ready, b + 1)
                pool.tensor_tensor(tx_tok[:, b], xn_tok[:, b], row_g2.unsqueeze(1).to_broadcast([P, TILES, D]),
                                   ALU.mult)
                link(pool.tensor_tensor(xn_tok[:, b], xn_tok[:, b],
                                        row_b2.unsqueeze(1).to_broadcast([P, TILES, D]), ALU.mult))
                pool.tensor_tensor(x_tok[:, b], x_tok[:, b], xn_tok[:, b], ALU.add).then_inc(mn_ready, 1)

            pool.memset(minus_half[:], -0.5).then_inc(pool_const, 1)
            pool.wait_ge(pool_const, 1)
            power(0, 0).then_inc(rstd0_ready, 1)
            pool.wait_ge(xn_ready, 1)
            norm_x(1)
            for b in range(BATCHES + 2):
                if b + 2 < BATCHES:
                    norm_x(b + 2)
                if b < BATCHES:
                    twist_x(b)
                if b >= 2:
                    rstd_of(1, b - 2)
                if b - 2 >= ACT_NORMS:
                    norm_x1(b - 2)
                if 3 <= b < BATCHES + 1:
                    scale_x1(b - 3)
            for j in range(PAIRS):
                s_pair(j)
            for b in (BATCHES - 2, BATCHES - 1):
                scale_x1(b)
            for j in range(PAIRS):
                scalars_2(j)
            for j in range(PAIRS):
                scalars_3(j)
                ax_pair(j)
            for b in range(BATCHES):
                gate_rows(b)
                if b == BATCHES - 1:
                    pool.wait_ge(mn_ready, b)
                    finish(BATCHES - 3)
                if b >= 1:
                    rstd_of(2, b - 1)
            for half, tiles in enumerate(HALVES):
                power(2, BATCHES - 1, tiles, half).then_inc(rstd_ready[2], 1)

        @block.scalar
        def _(act):
            def hi_x(b):
                act.wait_ge(xT_ps, b + 1)
                if b >= 2:
                    act.wait_ge(k_ps, TILES * (b - 1))
                act.activation(xT_hi[:, b % 2], ps_xT[:], ACT.Identity,
                               accum_out=sum_hi[:, b:b + 1]).then_inc(xT_hi_ready, 1)

            def exp_q(b):
                act.wait_ge(q_ps, b + 1)
                if b >= 2:
                    act.wait_ge(qf_ready, b - 1)
                act.activation(eq[:, b % 2], ps_q[:], ACT.Exp, bias=minus_one[:, 0:1]).then_inc(eq_ready, 1)

            def token_tile(n):
                act.wait_ge(k_ps, n + 1)
                if n >= 3:
                    act.wait_ge(kf_ready, n - 2)
                act.activation(ek[:, n % 3], ps_k[n % 3][:, 0:D], ACT.Exp, bias=minus_one[:, 0:1]).then_inc(ek_ready, 1)
                if n >= 3:
                    act.wait_ge(kv_ps, n - 2)
                act.copy(v1[:, n % 3, 0:D], ps_k[n % 3][:, D:2 * D]).then_inc(v_ready, 1)
                act.copy(pq[:, n].rearrange("p a d -> p (a d)"), ps_k[n % 3][:, 2 * D:4 * D]).then_inc(pq_ready, 1)

            def norm_1(b, tiles=range(TILES)):
                act.wait_ge(rstd_ready[1], b + 1)
                if b >= 2:
                    act.wait_ge(x1T_ps, b - 1)
                    act.wait_ge(x1g_ready, b - 1)
                for t in tiles:
                    last = act.activation(x1n[:, b % 2, t], u1[:, b % 2, t], ACT.Identity,
                                          scale=rstd[1][:, b, t:t + 1], bias=nmr[1][:, b, t:t + 1])
                if tiles[-1] == TILES - 1:
                    last.then_inc(x1n_ready, 1)

            def hi_x1(b):
                act.wait_ge(x1T_ps, b + 1)
                act.copy(x1_hi[:, b], ps_x1T[:]).then_inc(x1_hi_ready, 1)

            def global_act(i):
                act.wait_ge(gf_ps, i + 1)
                if i == 2:
                    act.activation(gt[:], ps_gf[:, 2], ACT.Tanh, scale=0.5, bias=half_gb3[:, 0:1]).then_inc(gf_act, 1)
                else:
                    m, dst, name = ((64, gh1, "gc_b1"), (32, gh2, "gc_b2"))[i]
                    act.activation(dst[0:m], ps_gf[0:m, i], ACT.Gelu, scale=1.0 / SEQ if i == 0 else 1.0,
                                   bias=col[0:m, COL[name]:COL[name] + 1]).then_inc(gf_act, 1)

            def gelu_1(s, pars=(0, 1)):
                for par in pars:
                    m = 2 * s + par
                    act.wait_ge(h1_ps, m + 1)
                    if s >= 2:
                        act.wait_ge(h2_ps, s - 1)
                    act.activation(h1[:, s % 2, par], ps_h1[par][:], ACT.Gelu,
                                   bias=col[:, COL["cn_b1"]:COL["cn_b1"] + 1]).then_inc(h1_ready, 1)

            def gelu_2(s):
                act.wait_ge(h2_ps, s + 1)
                if s >= 2:
                    act.wait_ge(h3_ps, s - 1)
                for ch in range(2):
                    cs = slice(ch * 256, (ch + 1) * 256)
                    act.activation(h2[:, s % 2, cs], ps_h2[s % 2][:, cs], ACT.Gelu,
                                   bias=col[:, COL["cn_b2"]:COL["cn_b2"] + 1]).then_inc(h2_ready, 1)

            def gelu_3(s):
                act.wait_ge(h3_ps, s + 1)
                if s >= 2:
                    act.wait_ge(z_ps, s - 1)
                act.activation(h3[:, s % 2], ps_h3, ACT.Gelu,
                               bias=col[:, COL["cn_b3"]:COL["cn_b3"] + 1]).then_inc(h3_ready, 1)

            def tanh_z(s):
                act.wait_ge(z_ps, s + 1)
                act.activation(tt[:, s].rearrange("p par (ch u) -> p u ch par", ch=2),
                               ps_z[:, s].rearrange("p (u ch par) -> p u ch par", u=2, ch=2), ACT.Tanh,
                               bias=half_b4[:, 0:1], scale=0.5).then_inc(tt_ready, 1)

            def silu_o(b):
                act.wait_ge(o_ready, b + 1)
                act.activation(xn_tok[:, b], xn_tok[:, b], ACT.Silu).then_inc(g_ready, 1)

            def silu_gate(n):
                b, c = divmod(n, CHUNKS)
                act.wait_ge(gate_ps, n + 1)
                if n >= 2:
                    act.wait_ge(hid_ready, n - 1)
                if n == 0:
                    act.wait_ge(bffn_ready, 1)
                m = CHUNK_ROWS[c]
                act.activation(sg[n % 2][0:m], ps_gate[n % 2][0:m], ACT.Silu,
                               bias=bffn[0:m, c:c + 1]).then_inc(sg_ready, 1)

            def norm_2(b):
                act.wait_ge(rstd_ready[2], b + 1)
                if b >= 2:
                    act.wait_ge(y_ready, b - 1)
                for t in range(TILES):
                    last = act.activation(un[b % 2][:, t], u2[b % 2][:, t], ACT.Identity,
                                          scale=rstd[2][:, b, t:t + 1], bias=nmr[2][:, b, t:t + 1])
                last.then_inc(un_ready, 1)

            act.wait_ge(small_loaded, 16)
            act.copy(eye_bf[:], eye).then_inc(eye_ready, 1)
            act.wait_ge(consts_ready, 1)
            act.wait_ge(sign_ready, 1)
            act.copy(first_hi[:], first_raw[:]).then_inc(first_hi_ready, 1)
            hi_x(0)
            for b in range(BATCHES):
                exp_q(b)
                for t in range(TILES):
                    token_tile(TILES * b + t)
                    if t in (0, 2) and b >= 3:
                        norm_1(b - 3, (t, t + 1))
                    if t == 1 and b + 1 < BATCHES:
                        hi_x(b + 1)
                if b >= 3:
                    hi_x1(b - 3)
            act.wait_ge(cols_ready, 1)
            global_act(0)
            gelu_1(0)
            global_act(1)
            gelu_1(1)
            global_act(2)
            for s in range(SLOTS - 2):
                gelu_2(s)
                if s in (0, 2, 4):
                    hi_x1(BATCHES - 3 + s // 2)
                if s >= 1:
                    tanh_z(s - 1)
                gelu_1(s + 2, (0,))
                gelu_3(s)
                gelu_1(s + 2, (1,))
            gelu_2(SLOTS - 2)
            tanh_z(SLOTS - 3)
            gelu_2(SLOTS - 1)
            gelu_3(SLOTS - 2)
            tanh_z(SLOTS - 2)
            gelu_3(SLOTS - 1)
            tanh_z(SLOTS - 1)
            for b in range(BATCHES + 1):
                if b < BATCHES:
                    silu_gate(CHUNKS * b)
                if b == 0:
                    silu_o(0)
                if b < BATCHES:
                    silu_gate(CHUNKS * b + 1)
                    silu_gate(CHUNKS * b + 2)
                if b >= 2:
                    norm_2(b - 2)
                if b + 1 < BATCHES:
                    silu_o(b + 1)

        @block.vector
        def _(dve):
            steps = [0]

            def mark(ins):
                steps[0] += 1
                ins.then_inc(dve_step, 1)
                return ins

            def link(ins):
                mark(ins)
                dve.wait_ge(dve_step, steps[0])

            def measure(i, b, src, tiles=range(TILES)):
                for t in tiles:
                    last = dve.bn_stats(st[i][:, b, t], src[:, t])
                last.then_inc(st_ready[i], 1)

            def moments(i, b, tiles=range(TILES), half=0):
                dve.wait_ge(st_ready[i], b + half + 1)
                for t in tiles:
                    last = dve.bn_aggr(mv[i][:, b, t], st[i][:, b, t])
                last.then_inc(mv_ready[i], 1)

            def negate_mean(i, b, tiles=range(TILES), half=0):
                dve.wait_ge(mv_ready[i], b + half + 1)
                ts = slice(tiles[0], tiles[-1] + 1)
                dve.tensor_scalar(nm[i][:, b, ts], mv[i][:, b, ts, 0], -1.0, None, ALU.mult).then_inc(mean_ready[i], 1)

            def stats(i, b, src):
                measure(i, b, src)
                moments(i, b)
                negate_mean(i, b)

            def stats_x(b):
                dve.wait_ge(x_loaded[b], 16)
                stats(0, b, x_tok[:, b])

            def norm_first(b):
                dve.wait_ge(rstd0_ready, 1)
                for t in range(TILES):
                    last = dve.tensor_scalar(xn_tok[:, b, t], x_tok[:, b, t], nm[0][:, b, t:t + 1],
                                             rstd[0][:, b, t:t + 1], ALU.add, ALU.mult)
                last.then_inc(xn_ready, 1)

            def lo_x(b):
                dve.wait_ge(xT_hi_ready, b + 1)
                if b >= 2:
                    dve.wait_ge(k_ps, TILES * (b - 1))
                dve.scalar_tensor_tensor(out=xT_lo[:, b % 2], in0=ps_xT[:], scalar=1.0,
                                         in1=xT_hi[:, b % 2].bitcast(F32), op0=ALU.mult, op1=ALU.subtract,
                                         accum_out=sum_lo[:, b:b + 1]).then_inc(xT_lo_ready, 1)

            def feature_q(b):
                dve.wait_ge(eq_ready, b + 1)
                if b >= 2:
                    dve.wait_ge(num_ps, b - 1)
                dve.scalar_tensor_tensor(out=qf[:, b % 2], in0=eq[:, b % 2], scalar=1.0, in1=ps_q[:],
                                         op0=ALU.min, op1=ALU.max).then_inc(qf_ready, 1)

            def feature_k(n):
                dve.wait_ge(pq_ready, n + 1)
                if n >= 3:
                    dve.wait_ge(kv_ps, n - 2)
                dve.scalar_tensor_tensor(out=kf[:, n % 3], in0=ek[:, n % 3], scalar=1.0, in1=ps_k[n % 3][:, 0:D],
                                         op0=ALU.min, op1=ALU.max).then_inc(kf_ready, 1)

            def copy_kv(b):
                dve.wait_ge(kv_ps, TILES * (b + 1))
                if b >= 2:
                    dve.wait_ge(num_ps, b - 1)
                dve.tensor_copy(kv_sb[:, b % 2], ps_kv[:, 0:D + 1]).then_inc(kv_ready, 1)

            def add_eps(b):
                dve.wait_ge(num_ps, b + 1)
                dve.tensor_scalar(den[:, b], ps_num[:, :, D], ATTN_EPS, None, ALU.add).then_inc(den_ready, 1)

            def invert_den(b):
                dve.wait_ge(den_ready, b + 1)
                dve.reciprocal(rden[:, b], den[:, b]).then_inc(rden_ready, 1)

            def attend(b):
                dve.wait_ge(rden_ready, b + 1)
                if b >= 2:
                    dve.wait_ge(x1n_ready, b - 1)
                for t in range(TILES):
                    last = dve.scalar_tensor_tensor(out=u1[:, b % 2, t], in0=ps_num[:, t, 0:D],
                                                    scalar=rden[:, b, t:t + 1], in1=xn_tok[:, b, t],
                                                    op0=ALU.mult, op1=ALU.add)
                last.then_inc(u1_ready, 1)

            def measure_u1(b):
                dve.wait_ge(u1_ready, b + 1)
                measure(1, b, u1[:, b % 2])

            def stats_u1(b):
                measure_u1(b)
                moments(1, b)
                negate_mean(1, b)

            def lo_x1(b):
                dve.wait_ge(x1_hi_ready, b + 1)
                dve.tensor_tensor(x1_lo[:, b], ps_x1T[:], x1_hi[:, b].bitcast(F32), ALU.subtract).then_inc(x1_lo_ready, 1)

            def coupling(s):
                j = s % PAIRS
                dve.wait_ge(tt_ready, s + 1)
                if s == 0:
                    dve.wait_ge(base_ready, 1)
                dve.scalar_tensor_tensor(out=cpl[:, s], in0=tt[:, s], scalar=gain[:, 1:2],
                                         in1=base[:, 2 * j:2 * j + 2].unsqueeze(2).to_broadcast([P, 2, TILES]),
                                         op0=ALU.mult, op1=ALU.add).then_inc(cpl_ready, 1)

            def next_r(s):
                cycle, j = divmod(s, PAIRS)
                dve.wait_ge(cpl_ready, s + 1)
                if cycle == 1:
                    dve.wait_ge(s_ready, j + 1)
                for i in range(2 * TILES):
                    n = 2 * TILES * j + i
                    ins = dve.scalar_tensor_tensor(out=r_tok[:, n], in0=pq[:, n, 1],
                                                    scalar=cpl[:, s, i // TILES, i % TILES:i % TILES + 1],
                                                    in1=pq[:, n, 0] if cycle == 0 else r_tok[:, n],
                                                    op0=ALU.mult, op1=ALU.add)
                    if i % TILES == TILES - 1:
                        ins.then_inc(r_ready, 1)

            def o3(b):
                j = b // 2
                dve.wait_ge(ax_ready, b + 1)
                for t in range(TILES):
                    i = TILES * (b % 2) + t
                    last = dve.scalar_tensor_tensor(out=xn_tok[:, b, t], in0=tx_tok[:, b, t],
                                                    scalar=ab[:, j, 3, i:i + 1], in1=xn_tok[:, b, t],
                                                    op0=ALU.mult, op1=ALU.add)
                last.then_inc(o_ready, 1)

            def hidden(n):
                b, c = divmod(n, CHUNKS)
                m = CHUNK_ROWS[c]
                dve.wait_ge(up_ps, n + 1)
                dve.wait_ge(sg_ready, n + 1)
                if b >= 2:
                    dve.wait_ge(down_ps, b - 1)
                dve.scalar_tensor_tensor(out=hid[b % 2][0:m, c], in0=ps_up[n % 2][0:m],
                                         scalar=bffn[0:m, CHUNKS + c:CHUNKS + c + 1], in1=sg[n % 2][0:m],
                                         op0=ALU.add, op1=ALU.mult).then_inc(hid_ready, 1)

            def residual_2(b):
                dve.wait_ge(down_ps, b + 1)
                dve.wait_ge(x1g_ready, b + 1)
                if b >= 2:
                    dve.wait_ge(un_ready, b - 1)
                dve.tensor_tensor(u2[b % 2], ps_down[b % 2][:].rearrange("p (t d) -> p t d", t=TILES), x1g[:, b],
                                  ALU.add).then_inc(u2_ready, 1)
                dve.wait_ge(u2_ready, b + 1)
                stats(2, b, u2[b % 2])

            def residual_last(half):
                b = BATCHES - 1
                dve.wait_ge(down_ps, BATCHES + half)
                if half == 0:
                    dve.wait_ge(x1g_ready, BATCHES)
                    dve.wait_ge(un_ready, b - 1)
                for t in HALVES[half]:
                    last = dve.tensor_tensor(u2[b % 2][:, t], ps_last[t][:, 0:D], x1g[:, b, t], ALU.add)
                last.then_inc(u2_ready, 1)

            def measure_last(half):
                dve.wait_ge(u2_ready, BATCHES + half)
                measure(2, BATCHES - 1, u2[(BATCHES - 1) % 2], HALVES[half])

            def finish(b):
                dve.wait_ge(un_ready, b + 1)
                dve.wait_ge(mn_ready, b + 1)
                if b >= 2:
                    dve.wait_ge(y_stored[b % 2], 16 * (b // 2))
                if b == BATCHES - 2:
                    dve.wait_ge(y_ready, b)
                link(dve.tensor_tensor(yb[b % 2], un[b % 2], tx_tok[:, b], ALU.mult))
                dve.tensor_tensor(yb[b % 2], yb[b % 2], x_tok[:, b], ALU.add).then_inc(y_ready, 1)

            def centre_last(half):
                b = BATCHES - 1
                dve.wait_ge(mean_ready[2], BATCHES + half)
                if half == 0:
                    dve.wait_ge(mn_ready, BATCHES)
                for t in HALVES[half]:
                    last = dve.scalar_tensor_tensor(out=u2[b % 2][:, t], in0=u2[b % 2][:, t],
                                                    scalar=nm[2][:, b, t:t + 1], in1=tx_tok[:, b, t],
                                                    op0=ALU.add, op1=ALU.mult)
                last.then_inc(centred, 1)

            def finish_last(half):
                b = BATCHES - 1
                dve.wait_ge(centred, half + 1)
                dve.wait_ge(rstd_ready[2], BATCHES + half)
                for t in HALVES[half]:
                    last = dve.scalar_tensor_tensor(out=u2[b % 2][:, t], in0=u2[b % 2][:, t],
                                                    scalar=rstd[2][:, b, t:t + 1], in1=x_tok[:, b, t],
                                                    op0=ALU.mult, op1=ALU.add)
                last.then_inc(y_ready, 1)

            def split_bias():
                dve.wait_ge(cols_loaded, 16)
                dve.tensor_scalar(bias_col[:, 0:2], col[:, 0:2], 1.0, None, ALU.add)
                dve.tensor_copy(bias_col[:, 2:3], col[:, 2:3])
                link(dve.tensor_tensor(bias_col[:, 3:4], col[:, 3:4], col[:, COL["b1"]:COL["b1"] + 1], ALU.add))
                for part in range(3):
                    last = dve.tensor_copy(bias_split[:, :, part], bias_col[:])
                    if part < 2:
                        link(last)
                        link(dve.tensor_tensor(bias_col[:], bias_col[:], bias_split[:, :, part], ALU.subtract))
                last.then_inc(split_ready, 1)

            dve.memset(minus_one[:], -1.0)
            dve.memset(bias3[:], 0.0)
            dve.memset(ones_bf[:], 1.0)
            dve.memset(v1[:, :, D:D + 1], 1.0)
            for i, s in enumerate((-1.0, 1.0, 1.0, -1.0)):
                last = dve.memset(sign[BLK * i:BLK * (i + 1)], s)
            last.then_inc(consts_ready, 1)
            dve.wait_ge(consts_ready, 1)
            stats_x(0)
            split_bias()
            dve.wait_ge(first_loaded, 16)
            dve.tensor_scalar(first_raw[:, 3 * D:4 * D], first_raw[:, 3 * D:4 * D], sign[:, 0:1], None,
                              ALU.mult).then_inc(sign_ready, 1)
            norm_first(0)
            dve.wait_ge(bias_ps, 1)
            dve.tensor_copy(bias3[0:3], ps_bias[0:3]).then_inc(bias_ready, 1)
            dve.wait_ge(x_loaded[1], 16)
            measure(0, 1, x_tok[:, 1])
            dve.wait_ge(first_hi_ready, 1)
            dve.tensor_tensor(first_lo[:], first_raw[:], first_hi[:].bitcast(F32), ALU.subtract).then_inc(first_ready, 1)
            moments(0, 1)
            negate_mean(0, 1)
            lo_x(0)
            dve.tensor_scalar(half_b4[:], col[:, COL["cn_b4"]:COL["cn_b4"] + 1], 0.5, None, ALU.mult)
            dve.tensor_scalar(half_gb3[:], col[:, COL["gc_b3"]:COL["gc_b3"] + 1], 0.5, None, ALU.mult)
            dve.tensor_scalar(gain[:, 0:1], col[:, COL["range"]:COL["range"] + 1], W_GLOBAL, None, ALU.mult)
            dve.tensor_scalar(gain[:, 1:2], col[:, COL["range"]:COL["range"] + 1], W_TOKEN, None,
                              ALU.mult).then_inc(cols_ready, 1)

            stats_x(2)
            for b in range(BATCHES):
                if b >= 2:
                    add_eps(b - 2)
                feature_q(b)
                if b >= 2:
                    invert_den(b - 2)
                feature_k(TILES * b)
                if b == BATCHES - 1:
                    dve.wait_ge(xT_lo_ready, BATCHES)
                    dve.tensor_tensor(ctx_sum[:], sum_hi[:], sum_lo[:], ALU.add).then_inc(ctx_ready, 1)
                if b >= 1:
                    copy_kv(b - 1)
                if b >= 2:
                    attend(b - 2)
                feature_k(TILES * b + 1)
                if b + 1 < BATCHES:
                    lo_x(b + 1)
                if b >= 2:
                    measure_u1(b - 2)
                feature_k(TILES * b + 2)
                if b >= 2:
                    moments(1, b - 2)
                feature_k(TILES * b + 3)
                if b >= 2:
                    negate_mean(1, b - 2)
                if b + 3 < BATCHES:
                    dve.wait_ge(x_loaded[b + 3], 16)
                    measure(0, b + 3, x_tok[:, b + 3])
                if 3 <= b < BATCHES - 1:
                    lo_x1(b - 3)
                if b + 3 < BATCHES:
                    moments(0, b + 3)
                    negate_mean(0, b + 3)
                if b == 1:
                    dve.wait_ge(ffn_loaded, 16)
                    dve.tensor_scalar(ffn_scaled[:], ffn_raw[:], col[:, COL["g1"]:COL["g1"] + 1], None,
                                      ALU.mult).then_inc(ffn_step, 1)
                if b == 5:
                    dve.wait_ge(ffn_step, 1)
                    dve.tensor_copy(ffn_hi[:], ffn_scaled[:]).then_inc(ffn_step, 1)
                if b == 6:
                    dve.wait_ge(ffn_step, 2)
                    dve.tensor_tensor(ffn_lo[:], ffn_scaled[:], ffn_hi[:].bitcast(F32),
                                      ALU.subtract).then_inc(ffn_ready, 1)
            add_eps(BATCHES - 2)
            invert_den(BATCHES - 2)
            copy_kv(BATCHES - 1)
            attend(BATCHES - 2)
            lo_x1(BATCHES - 4)
            stats_u1(BATCHES - 2)
            add_eps(BATCHES - 1)
            invert_den(BATCHES - 1)
            attend(BATCHES - 1)
            dve.wait_ge(bffn_ps, 1)
            for c, m in enumerate(CHUNK_ROWS):
                last = dve.tensor_tensor(bffn[0:m, c::CHUNKS], ps_bf[0:m, c::CHUNKS],
                                         col[0:m, COL["bg0"] + c::CHUNKS], ALU.add)
            last.then_inc(bffn_ready, 1)
            stats_u1(BATCHES - 1)
            lo_x1(BATCHES - 3)
            dve.wait_ge(gf_act, 3)
            dve.tensor_scalar(base[:], gt[:], gain[:, 0:1], BASE_COUPLING, ALU.mult, ALU.add).then_inc(base_ready, 1)
            for s in range(SLOTS):
                coupling(s)
                if s < 2 * PAIRS:
                    next_r(s)
                    if s in (1, 3):
                        lo_x1(BATCHES - 2 + s // 2)
                if s == SLOTS - 2:
                    o3(0)
            for b in range(BATCHES):
                hidden(CHUNKS * b)
                if b >= 3:
                    finish(b - 3)
                hidden(CHUNKS * b + 1)
                if b + 1 < BATCHES:
                    o3(b + 1)
                hidden(CHUNKS * b + 2)
                if b >= 1:
                    residual_2(b - 1)
            last = BATCHES - 1
            residual_last(0)
            measure_last(0)
            residual_last(1)
            moments(2, last, HALVES[0])
            measure_last(1)
            negate_mean(2, last, HALVES[0])
            moments(2, last, HALVES[1], half=1)
            negate_mean(2, last, HALVES[1], half=1)
            for half in range(2):
                centre_last(half)
            finish(last - 1)
            for half in range(2):
                finish_last(half)

        @block.tensor
        def _(pe):
            def transposes(dst, src):
                for t in range(TILES):
                    last = pe.transpose(dst[:, t * P:(t + 1) * P], src[:, t], eye)
                return last

            def transpose_x(b):
                pe.wait_ge(xn_ready, b + 1)
                if b >= 1:
                    pe.wait_ge(xT_lo_ready, b)
                if b >= 5:
                    pe.wait_ge(x1_lo_ready, b - 4)
                transposes(ps_xT, xn_tok[:, b]).then_inc(xT_ps, 1)

            def project_q(b):
                pe.wait_ge(xT_hi_ready, b + 1)
                if b == 0:
                    pe.wait_ge(first_ready, 1)
                    pe.wait_ge(bias_ready, 1)
                if b >= 1:
                    pe.wait_ge(qf_ready, b)
                hi, lo = xT_hi[:, b % 2], xT_lo[:, b % 2]
                wq = slice(4 * D, 5 * D)
                pe.matmul(ps_q[:], first_hi[:, wq], hi, start=True, stop=False)
                pe.matmul(ps_q[:], first_lo[:, wq], hi, start=False, stop=False)
                pe.matmul(ps_q[:], bias3[:, 0:D], ones_bf[:], start=False, stop=False)
                pe.wait_ge(xT_lo_ready, b + 1)
                pe.matmul(ps_q[:], first_hi[:, wq], lo, start=False, stop=True).then_inc(q_ps, 1)

            def project_tokens(n):
                b, t = divmod(n, TILES)
                if n >= 3:
                    pe.wait_ge(kf_ready, n - 2)
                dst = ps_k[n % 3]
                hi, lo = xT_hi[:, b % 2, t * P:(t + 1) * P], xT_lo[:, b % 2, t * P:(t + 1) * P]
                pe.matmul(dst[:], hi, first_hi[:, 0:4 * D], start=True, stop=False)
                pe.matmul(dst[:], hi, first_lo[:, 0:4 * D], start=False, stop=False)
                pe.matmul(dst[:, 0:2 * D], ones_bf[:, 0:P], bias3[:, D:3 * D], start=False, stop=False)
                pe.matmul(dst[:], lo, first_hi[:, 0:4 * D], start=False, stop=True).then_inc(k_ps, 1)

            def sum_kv(n):
                b, t = divmod(n, TILES)
                pe.wait_ge(kf_ready, n + 1)
                pe.wait_ge(v_ready, n + 1)
                if t == 0 and b >= 1:
                    pe.wait_ge(kv_ready, b)
                pe.matmul(ps_kv[:, 0:D + 1], kf[:, n % 3], v1[:, n % 3], start=(t == 0),
                          stop=(t == TILES - 1)).then_inc(kv_ps, 1)

            def numerator(b):
                pe.wait_ge(kv_ready, b + 1)
                pe.wait_ge(qf_ready, b + 1)
                if b >= 1:
                    pe.wait_ge(u1_ready, b)
                for t in range(TILES):
                    last = pe.matmul(ps_num[:, t, 0:D + 1], qf[:, b % 2, t * P:(t + 1) * P], kv_sb[:, b % 2],
                                     start=True, stop=True)
                last.then_inc(num_ps, 1)

            def transpose_x1(b):
                pe.wait_ge(x1n_ready, b + 1)
                if b >= 1:
                    pe.wait_ge(x1_lo_ready, b)
                pe.wait_ge(xT_lo_ready, min(b + 5, BATCHES))
                transposes(ps_x1T, x1n[:, b % 2]).then_inc(x1T_ps, 1)

            def layer_1(s, pars=(0, 1)):
                cycle, j = divmod(s, PAIRS)
                for par in pars:
                    m = 2 * s + par
                    if cycle >= 1:
                        pe.wait_ge(r_ready, m - 2 * PAIRS + 1)
                    if m >= 2:
                        pe.wait_ge(h1_ready, m - 1)
                    n0 = 2 * TILES * j + TILES * par
                    src = pq[:, n0:n0 + TILES, 0] if cycle == 0 else r_tok[:, n0:n0 + TILES]
                    transposes(ps_h1[par], src).then_inc(h1_ps, 1)

            def layer_2(s):
                pe.wait_ge(h1_ready, 2 * s + 2)
                if s >= 2:
                    pe.wait_ge(h2_ready, 2 * (s - 1))
                for par in range(2):
                    last = pe.matmul(ps_h2[s % 2][64 * par:64 * par + 64, :], sm("cn_w2"), h1[:, s % 2, par],
                                     start=True, stop=True)
                last.then_inc(h2_ps, 1)

            def layer_3(s):
                if s == 0:
                    pe.wait_ge(bffn_ready, 1)
                else:
                    pe.wait_ge(h3_ready, s)
                for ch in range(2):
                    pe.wait_ge(h2_ready, 2 * s + ch + 1)
                    last = pe.matmul(ps_h3[64 * ch:64 * ch + 64, :], sm("cn_w3"),
                                     h2[:, s % 2, ch * 256:(ch + 1) * 256], start=True, stop=True)
                last.then_inc(h3_ps, 1)

            def layer_4(s):
                pe.wait_ge(h3_ready, s + 1)
                if s == 0:
                    pe.wait_ge(u1_ready, BATCHES)
                else:
                    pe.wait_ge(tt_ready, s)
                for u in range(2):
                    last = pe.matmul(ps_z[:, s, 4 * u:4 * u + 4], h3[:, s % 2, u * P:(u + 1) * P], sm("cn_w4"),
                                     start=True, stop=True)
                last.then_inc(z_ps, 1)

            def global_layer(i):
                if i == 0:
                    pe.wait_ge(ctx_ready, 1)
                    pe.matmul(ps_gf[0:64, 0], sm("gc_w1"), ctx_sum[:], start=True, stop=True).then_inc(gf_ps, 1)
                else:
                    pe.wait_ge(gf_act, i)
                    k, m, src, w = ((64, 32, gh1, "gc_w2"), (32, P, gh2, "gc_w3"))[i - 1]
                    pe.matmul(ps_gf[0:m, i], sm(w, k), src[0:k], start=True, stop=True).then_inc(gf_ps, 1)

            def ffn_bias():
                pe.wait_ge(ffn_loaded, 16)
                pe.wait_ge(cols_loaded, 16)
                pe.wait_ge(kv_ready, BATCHES)
                for i in range(2 * CHUNKS):
                    k, c = divmod(i, CHUNKS)
                    m = CHUNK_ROWS[c]
                    last = pe.matmul(ps_bf[0:m, i:i + 1], ffn_raw[:, k * HID + c * P:k * HID + c * P + m],
                                     col[:, COL["b1"]:COL["b1"] + 1], start=True, stop=True)
                last.then_inc(bffn_ps, 1)

            def gate_up(n, parts=(0, 1)):
                b, c = divmod(n, CHUNKS)
                m = CHUNK_ROWS[c]
                if n >= 2 and 0 in parts:
                    pe.wait_ge(sg_ready, n - 1)
                for k in parts:
                    dst, done = ((ps_gate, gate_ps), (ps_up, up_ps))[k]
                    if k == 1 and n >= 2:
                        pe.wait_ge(hid_ready, n - 1)
                    w = slice(k * HID + c * P, k * HID + c * P + m)
                    pe.matmul(dst[n % 2][0:m], ffn_hi[:, w], x1_hi[:, b], start=True, stop=False)
                    pe.matmul(dst[n % 2][0:m], ffn_hi[:, w], x1_lo[:, b], start=False, stop=False)
                    pe.matmul(dst[n % 2][0:m], ffn_lo[:, w], x1_hi[:, b], start=False, stop=True).then_inc(done, 1)

            def down(b, tiles):
                pe.wait_ge(hid_ready, CHUNKS * (b + 1))
                if b >= 2:
                    pe.wait_ge(u2_ready, b - 1)
                dst = ps_down[b % 2]
                for t in tiles:
                    pe.matmul(dst[:, t * P:(t + 1) * P], ones_bf[:, 0:P], bias3[:, 3 * D:4 * D], start=True, stop=False)
                    for c, m in enumerate(CHUNK_ROWS):
                        last = pe.matmul(dst[:, t * P:(t + 1) * P], hid[b % 2][0:m, c, t * P:(t + 1) * P],
                                         wd[0:m, c], start=False, stop=(c == CHUNKS - 1))
                if tiles[-1] == TILES - 1:
                    last.then_inc(down_ps, 1)

            def down_last():
                b = BATCHES - 1
                for t in range(TILES):
                    if t == 0:
                        pe.wait_ge(u2_ready, b - 1)
                    if t == 2:
                        pe.wait_ge(hid_ready, CHUNKS * (b + 1) - 1)
                    pe.matmul(ps_last[t][:, 0:D], ones_bf[:, 0:P], bias3[:, 3 * D:4 * D], start=True, stop=False)
                    for c in range(CHUNKS - 1):
                        pe.wait_ge(hid_ready, CHUNKS * b + c + 1)
                        m = CHUNK_ROWS[c]
                        pe.matmul(ps_last[t][:, 0:D], hid[b % 2][0:m, c, t * P:(t + 1) * P], wd[0:m, c],
                                  start=False, stop=False)
                pe.wait_ge(hid_ready, CHUNKS * (b + 1))
                c = CHUNKS - 1
                m = CHUNK_ROWS[c]
                for tiles in HALVES:
                    for t in tiles:
                        last = pe.matmul(ps_last[t][:, 0:D], hid[b % 2][0:m, c, t * P:(t + 1) * P], wd[0:m, c],
                                         start=False, stop=True)
                    last.then_inc(down_ps, 1)

            pe.wait_ge(small_loaded, 16)
            pe.wait_ge(eye_ready, 1)
            pe.wait_ge(split_ready, 1)
            for i in range(4):
                last = pe.transpose(ps_bias[0:3, i * D:(i + 1) * D], bias_split[:, i, 0:3], eye_bf[:])
            last.then_inc(bias_ps, 1)
            transpose_x(0)
            for b in range(BATCHES):
                project_q(b)
                for t in range(TILES):
                    n = TILES * b + t
                    project_tokens(n)
                    if n >= 2:
                        sum_kv(n - 2)
                    if t == 1 and b + 1 < BATCHES:
                        transpose_x(b + 1)
                    if t == 3 and b >= 1:
                        numerator(b - 1)
                    if t == 3 and b >= 3:
                        transpose_x1(b - 3)
            sum_kv(NTILE - 2)
            sum_kv(NTILE - 1)
            pe.wait_ge(qf_ready, BATCHES)
            global_layer(0)
            pe.wait_ge(kf_ready, NTILE)
            layer_1(0)
            global_layer(1)
            ffn_bias()
            numerator(BATCHES - 1)
            layer_1(1)
            global_layer(2)
            for s in range(SLOTS - 2):
                if s == 1:
                    pe.wait_ge(gf_act, 3)
                layer_2(s)
                if s in (0, 2, 4):
                    transpose_x1(BATCHES - 3 + s // 2)
                if s >= 1:
                    layer_4(s - 1)
                layer_1(s + 2, (0,))
                layer_3(s)
                layer_1(s + 2, (1,))
            layer_2(SLOTS - 2)
            layer_4(SLOTS - 3)
            layer_2(SLOTS - 1)
            pe.wait_ge(h1_ready, 2 * SLOTS)
            pe.wait_ge(ffn_ready, 1)
            pe.wait_ge(x1_lo_ready, BATCHES)
            layer_3(SLOTS - 2)
            gate_up(0, (0,))
            layer_4(SLOTS - 2)
            layer_3(SLOTS - 1)
            gate_up(0, (1,))
            layer_4(SLOTS - 1)
            gate_up(1)
            pe.wait_ge(h2_ready, 2 * SLOTS)
            pe.wait_ge(down_loaded, 16)
            for b in range(BATCHES):
                for c in range(CHUNKS):
                    if CHUNKS * b + c >= 2:
                        gate_up(CHUNKS * b + c)
                    if b >= 1 and c >= 1:
                        down(b - 1, (2 * c - 2, 2 * c - 1))
            down_last()


def kernel(**inputs):
    import numpy as np
    import concourse.bacc as bacc
    from concourse.bass_utils import run_bass_kernel_spmd

    a = {k: np.asarray(v) for k, v in inputs.items()}
    w = {k.split("_", 2)[2]: v for k, v in a.items() if k.startswith("L0_ffn")}
    t = {k.split("_", 2)[2]: v for k, v in a.items() if k.startswith("L0_attn")}
    f32 = np.float32

    def padded(v, rows, at=0):
        out = np.zeros((rows,) + v.shape[1:], f32)
        out[at:at + v.shape[0]] = v
        return out

    wqkv = t["Wqkv"]
    w_first = np.concatenate([wqkv[:, D:3 * D], w["cn_w1"],
                              np.concatenate([w["cn_w1"][2 * BLK:], w["cn_w1"][:2 * BLK]]), wqkv[:, 0:D]], axis=1)
    w3 = np.zeros((P, 64), f32)
    w4 = np.zeros((P, 4), f32)
    for i in range(2):
        w3[64 * i:64 * i + 64, 32 * i:32 * i + 32] = w["cn_w3"]
    for i in range(4):
        w4[32 * i:32 * i + 32, i:i + 1] = w["cn_w4"]
    w_small = np.concatenate([w["cn_w2"], w3, w4, w["gc_w1"], padded(w["gc_w2"], P),
                              padded(np.repeat(w["gc_w3"], P, axis=1), P), np.eye(P, dtype=f32)], axis=1)
    w_ffn = np.concatenate([t["Wg"], t["Wu"]], axis=1)
    w_down = padded(t["Wd"], CHUNKS * P).reshape(CHUNKS, P, D).transpose(1, 0, 2)
    cols = [w["cn_b1"], np.tile(w["cn_b2"], 2), np.tile(w["cn_b3"], 4), np.repeat(w["cn_b4"], P),
            np.repeat(w["adaptive_range"], P), padded(w["gc_b1"], P), padded(w["gc_b2"], P),
            np.repeat(w["gc_b3"], P), t["g1"], t["b1"]]
    cols = list(t["bqkv"].reshape(3, D)) + [t["bd"]] + cols
    for name in ("bg", "bu"):
        cols += list(padded(t[name], CHUNKS * P).reshape(CHUNKS, P))
    rows = np.concatenate([t["g1"], t["g2"], t["b2"]])[None]
    sent = {"x": t["x"], "w_first": w_first, "w_small": w_small, "w_ffn": w_ffn, "w_down": w_down,
            "cols": np.stack(cols, axis=1), "rows": rows}

    nc = bacc.Bacc("TRN2", target_bir_lowering=False, num_devices=1)
    arrays, args = {}, []
    for name, v in sent.items():
        v = np.ascontiguousarray(v)
        arrays[f"in_{name}"] = v
        args.append(nc.dram_tensor(f"in_{name}", v.shape, mybir.dt.from_np(v.dtype), kind="ExternalInput").ap())
    out = nc.dram_tensor("out", sent["x"].shape, F32, kind="ExternalOutput").ap()
    gated_block(nc, *args, out)
    result = run_bass_kernel_spmd(nc, [arrays], core_ids=[0])
    return result.results[0]["out"]
```
